# Optimizing a Trainium2 kernel written in Bass

```python
import numpy as np
import jax
import jax.numpy as jnp

def _softmax(x, axis=-1):
    return jax.nn.softmax(x, axis=axis)

def _gelu(x):
    return jax.nn.gelu(x, approximate=True)

def _silu(x):
    return jax.nn.silu(x)

def _sigmoid(x):
    return jax.nn.sigmoid(x)

def _layernorm(x, axis=-1, eps=1e-05):
    m = jnp.mean(x, axis=axis, keepdims=True)
    v = jnp.var(x, axis=axis, keepdims=True)
    return (x - m) / jnp.sqrt(v + eps)

def _scatter_add(tgt, idx, src, axis=0):
    return tgt.at[idx].add(src)

def _segment_sum(src, seg, n):
    return jax.ops.segment_sum(src, seg, n)
kernel_name = 'mk_flamingo_gated_d1_seqx_r4_3ddd8d'

def setup_inputs(seed: int=0):
    np.random.seed(seed)
    _w = jnp.asarray

    def _rec_inputs():
        import jax
        import jax.numpy as jnp
        _rk = jax.random.key(seed)
        x = 7.22e-05 + 1 * jax.random.normal(jax.random.fold_in(_rk, 1), (4, 512, 512), jnp.float32)
        _lenS = 512 - jax.random.randint(jax.random.fold_in(_rk, 7), (4,), 0, max(1, 512 // 4) + 1, jnp.int32)
        _lenS2 = 1601 - jax.random.randint(jax.random.fold_in(_rk, 8), (4,), 0, max(1, 1601 // 4) + 1, jnp.int32)
        _ctx_2048P = jax.random.normal(jax.random.fold_in(_rk, 11), (4, 16, 512), jnp.float32)
        _ctx_2048c = jax.random.dirichlet(jax.random.fold_in(_rk, 511), 0.3 * jnp.ones((16,), jnp.float32), (4, 1601))
        _ctx_2048t = jnp.einsum('bsk,bkd->bsd', _ctx_2048c, _ctx_2048P)
        _ctx_2048t = _ctx_2048t * jax.lax.rsqrt(jnp.mean(jnp.square(_ctx_2048t)) + 1e-12) * 0.953939
        ctx_2048 = 4.13588e-05 + 0.999923 * (_ctx_2048t + 0.3 * jax.random.normal(jax.random.fold_in(_rk, 611), (4, 1601, 512), jnp.float32))
        _g = jax.random.normal(jax.random.fold_in(_rk, 9001), (2, 1), jnp.float32)
        _g = jnp.sign(_g) * jnp.maximum(jnp.abs(_g), 1.0) + (_g == 0) * 1.0
        g_xattn = _g[0]
        g_ffn = _g[1]
        return (x, ctx_2048, g_xattn, g_ffn)
    x, ctx_2048, g_xattn, g_ffn = _rec_inputs()

    def _L0_xattn_setup():
        import math
        import jax, jax.numpy as jnp
        import numpy as np
        HEADS = 16
        MASKED_BIAS = -10000.0

        def _mha(q, k, v):
            B, Sq, D = q.shape
            Sk = k.shape[-2]
            hd = D // HEADS
            qh = q.reshape(B, Sq, HEADS, hd).transpose(0, 2, 1, 3)
            kh = k.reshape(B, Sk, HEADS, hd).transpose(0, 2, 1, 3)
            vh = v.reshape(B, Sk, HEADS, hd).transpose(0, 2, 1, 3)
            scores = jnp.einsum('bhqd,bhkd->bhqk', qh, kh) / math.sqrt(hd)
            qi = jnp.arange(Sq)[:, None] + (Sk - Sq)
            ki = jnp.arange(Sk)[None, :]
            causal = ki <= qi
            scores = jnp.where(causal[None, None], scores, jnp.asarray(MASKED_BIAS, scores.dtype))
            attn = jax.nn.softmax(scores, axis=-1)
            out = jnp.einsum('bhqk,bhkd->bhqd', attn, vh)
            return out.transpose(0, 2, 1, 3).reshape(B, Sq, D)
        key = jax.random.key(seed)
        kq, kk, kv = jax.random.split(key, 3)
        B, S, D = (4, 256, 512)
        q = jax.random.normal(kq, (B, S, D), dtype=jnp.float32)
        k = jax.random.normal(kk, (B, S, D), dtype=jnp.float32)
        v = jax.random.normal(kv, (B, S, D), dtype=jnp.float32)
        return {'q': q, 'k': k, 'v': v}
    _L0_xattn_all = _L0_xattn_setup()
    _L0_xattn_in = {k: v for k, v in _L0_xattn_all.items() if k in ()}
    del _L0_xattn_all

    def _L0_ffn_setup():
        import jax, jax.numpy as jnp
        import numpy as np
        FP8_MAX = 448.0
        GLOBAL_DIV = 448.0 * 6.0

        def _fp8(x):
            return x.astype(jnp.float8_e4m3fn).astype(jnp.float32)

        def _reorder_quantize_x(x, idx):
            scale = jnp.max(jnp.abs(x)) / GLOBAL_DIV
            xr = (x / scale)[:, idx]
            scale_x = jnp.max(jnp.abs(xr), axis=1, keepdims=True) / FP8_MAX
            qx = _fp8(xr / scale_x)
            return (qx, scale_x, scale)

        def _qlinear(qx, scale_x, scale, W, idx, out_idx=None):
            Wr = W[:, idx]
            w_scale = jnp.max(jnp.abs(Wr), axis=1, keepdims=True) / FP8_MAX
            qw = _fp8(Wr / w_scale)
            y = qx * scale_x @ (qw * w_scale).T * scale
            if out_idx is not None:
                y = y[:, out_idx]
            return y
        key = jax.random.key(seed)
        ks = jax.random.split(key, 6)
        B, S, H, I = (2, 256, 512, 1408)
        return {'x': jax.random.normal(ks[0], (B, S, H), jnp.float32), 'w_gate': jax.random.normal(ks[1], (I, H), jnp.float32) * 0.02, 'w_up': jax.random.normal(ks[2], (I, H), jnp.float32) * 0.02, 'w_down': jax.random.normal(ks[3], (H, I), jnp.float32) * 0.02, 'up_reorder_index': jax.random.permutation(ks[4], jnp.arange(H, dtype=jnp.int64)), 'down_reorder_index': jax.random.permutation(ks[5], jnp.arange(I, dtype=jnp.int64))}
    _L0_ffn_all = _L0_ffn_setup()
    _L0_ffn_in = {k: v for k, v in _L0_ffn_all.items() if k in ('w_gate', 'w_up', 'w_down', 'up_reorder_index', 'down_reorder_index')}
    del _L0_ffn_all
    return {'x': x, 'ctx_2048': ctx_2048, 'g_xattn': g_xattn, 'g_ffn': g_ffn, 'L0_ffn_w_gate': _L0_ffn_in['w_gate'], 'L0_ffn_w_up': _L0_ffn_in['w_up'], 'L0_ffn_w_down': _L0_ffn_in['w_down'], 'L0_ffn_up_reorder_index': _L0_ffn_in['up_reorder_index'], 'L0_ffn_down_reorder_index': _L0_ffn_in['down_reorder_index']}

def reference(x, ctx_2048, g_xattn, g_ffn, L0_ffn_w_gate, L0_ffn_w_up, L0_ffn_w_down, L0_ffn_up_reorder_index, L0_ffn_down_reorder_index):
    import jax
    import jax.numpy as jnp

    def _L0_xattn_ref(q, k, v):
        import math
        import jax, jax.numpy as jnp
        import numpy as np
        HEADS = 16
        MASKED_BIAS = -10000.0

        def _mha(q, k, v):
            B, Sq, D = q.shape
            Sk = k.shape[-2]
            hd = D // HEADS
            qh = q.reshape(B, Sq, HEADS, hd).transpose(0, 2, 1, 3)
            kh = k.reshape(B, Sk, HEADS, hd).transpose(0, 2, 1, 3)
            vh = v.reshape(B, Sk, HEADS, hd).transpose(0, 2, 1, 3)
            scores = jnp.einsum('bhqd,bhkd->bhqk', qh, kh) / math.sqrt(hd)
            qi = jnp.arange(Sq)[:, None] + (Sk - Sq)
            ki = jnp.arange(Sk)[None, :]
            causal = ki <= qi
            scores = jnp.where(causal[None, None], scores, jnp.asarray(MASKED_BIAS, scores.dtype))
            attn = jax.nn.softmax(scores, axis=-1)
            out = jnp.einsum('bhqk,bhkd->bhqd', attn, vh)
            return out.transpose(0, 2, 1, 3).reshape(B, Sq, D)
        return _mha(q, k, v)

    def _L0_ffn_ref(x, w_gate, w_up, w_down, up_reorder_index, down_reorder_index):
        import jax, jax.numpy as jnp
        import numpy as np
        FP8_MAX = 448.0
        GLOBAL_DIV = 448.0 * 6.0

        def _fp8(x):
            return x.astype(jnp.float8_e4m3fn).astype(jnp.float32)

        def _reorder_quantize_x(x, idx):
            scale = jnp.max(jnp.abs(x)) / GLOBAL_DIV
            xr = (x / scale)[:, idx]
            scale_x = jnp.max(jnp.abs(xr), axis=1, keepdims=True) / FP8_MAX
            qx = _fp8(xr / scale_x)
            return (qx, scale_x, scale)

        def _qlinear(qx, scale_x, scale, W, idx, out_idx=None):
            Wr = W[:, idx]
            w_scale = jnp.max(jnp.abs(Wr), axis=1, keepdims=True) / FP8_MAX
            qw = _fp8(Wr / w_scale)
            y = qx * scale_x @ (qw * w_scale).T * scale
            if out_idx is not None:
                y = y[:, out_idx]
            return y
        B, S, H = x.shape
        xf = x.reshape(B * S, H)
        qx, sx, sc = _reorder_quantize_x(xf, up_reorder_index)
        g = _qlinear(qx, sx, sc, w_gate, up_reorder_index, out_idx=down_reorder_index)
        u = _qlinear(qx, sx, sc, w_up, up_reorder_index, out_idx=down_reorder_index)
        t = jax.nn.silu(g) * u
        qt, st, sct = _reorder_quantize_x(t, down_reorder_index)
        y = _qlinear(qt, st, sct, w_down, down_reorder_index)
        return y.reshape(B, S, H)
    x = x + jnp.tanh(g_xattn[0]) * _L0_xattn_ref(_layernorm(x, axis=-1), ctx_2048, ctx_2048)
    x = x + jnp.tanh(g_ffn[0]) * _L0_ffn_ref(_layernorm(x, axis=-1), L0_ffn_w_gate, L0_ffn_w_up, L0_ffn_w_down, L0_ffn_up_reorder_index, L0_ffn_down_reorder_index)
    return x

_drawn_inputs = setup_inputs


def setup_inputs(seed=0):
    import zlib

    import numpy as np

    out = dict(_drawn_inputs(seed))
    spreads = {}
    factors = {}
    for name, (base, spread) in spreads.items():
        noise = np.random.default_rng([zlib.crc32(name.encode()), seed]).standard_normal(out[name].shape)
        drawn = base * np.exp(spread * noise) if base else spread * noise
        out[name] = jnp.asarray(drawn.astype(out[name].dtype))
    for name, factor in factors.items():
        out[name] = (out[name] * factor).astype(out[name].dtype)
    return out
```

```python
import concourse.bass as bass
from concourse import mybir
from contextlib import ExitStack


def flamingo_gated_block(nc, x_d, ctx_d, gx_d, gf_d, wg_d, wu_d, wd_d, didx_d, out_d):
    nc.disable_value_cache = True
    f32, f16, bf16, i32 = mybir.dt.float32, mybir.dt.float16, mybir.dt.bfloat16, mybir.dt.int32
    ALU = mybir.AluOpType
    ACT = mybir.ActivationFunctionType
    AX = mybir.AxisListType

    B, S, D = x_d.shape
    SK = ctx_d.shape[1]
    I = wg_d.shape[0]
    P = 128
    H = 16
    HD = D // H
    SCALE = HD ** -0.5
    MASKED = -10000.0
    QT = S // P
    NG, GH = 4, 4
    NEAR = SK - S
    NF = 9
    FL = NEAR // NF
    NT = NF + QT
    KT = [(FL * t, FL) for t in range(NF)] + [(NEAR + P * i, P) for i in range(QT)]
    ST = 3 * HD + 1
    IT = I // P
    DC = D // P
    GC = 4
    CW = I // GC
    FP8_MAX = 448.0
    EXP_BITS = 0x7F800000
    MIN_EXP, ROUND = 2.0 ** -6, 1.5 * 2.0 ** 20
    NEG = -1.0e30
    EPS = 1e-5
    UNITS = GH * NT
    CH = 52
    assert NF * FL == NEAR and IT * P == I

    chunks = []
    for hh in range(GH):
        for qt in range(QT):
            end = NEAR + P * (qt + 1)
            for c in range((end + 511) // 512):
                chunks.append((hh, qt, c, 512 * c, min(512 * c + 512, end)))
    assert len(chunks) == CH

    with ExitStack() as ctx:
        def sb(name, shape, dt=f32):
            return ctx.enter_context(nc.sbuf_tensor(name, shape, dt))

        def sem(name):
            return ctx.enter_context(nc.semaphore(name))

        idf = sb("idf", [P, P])
        idh = sb("idh", [P, P], f16)
        idb = sb("idb", [P, P], bf16)
        onesf = sb("onesf", [P, P])
        later = sb("later", [P, P])
        maskT = sb("maskT", [P, P], bf16)
        floor = sb("floor", [P, GH, QT])
        count = sb("count", [P, QT])
        cneg = sb("cneg", [P, 1])
        half = sb("half", [P, QT])
        gates = sb("gates", [1, 2])
        tg = sb("tg", [P, 2])
        idx = sb("idx", [P, IT], i32)
        wgu = sb("wgu", [P, DC, 2 * I], bf16)
        wdn = sb("wdn", [P, IT, D], bf16)
        wsb = sb("wsb", [P, 2 * I])
        wdb = sb("wdb", [P, D])
        xs = sb("xs", [P, QT, D])
        ctxt = sb("ctxt", [P, NT, D])
        vst = sb("vst", [P, NT, H, HD + 1])
        kTh = sb("kTh", [P, NG, SK], f16)
        kTl = sb("kTl", [P, NG, SK], f16)
        qTh = sb("qTh", [P, NG, S], f16)
        qTl = sb("qTl", [P, NG, S], f16)
        kst = [sb(f"kst{i}", [ST, GH, SK], f16) for i in range(2)]
        qst = [sb(f"qst{i}", [ST, GH, S], f16) for i in range(2)]
        suf = sb("suf", [P, QT, D])
        NP = 3
        pr = sb("pr", [P, NP, S])
        oT = sb("oT", [HD + 1, S])
        xl = sb("xl", [P, 2, D])
        stat = sb("stat", [P, QT, 6])
        mv = sb("mv", [P, QT, 2])
        ve = sb("ve", [P, QT])
        rstd = sb("rstd", [P, QT])
        mch = sb("mch", [P, GH, QT, 4])
        mg = sb("mg", [P, GH, QT])
        m16 = sb("m16", [P, 2, GH, QT], f16)
        mrow = sb("mrow", [GH, 2, S], f16)
        w = sb("w", [P, 2, GH, QT])
        cmb = sb("cmb", [P, 2, QT, HD])
        den = sb("den", [P, 3, QT])
        qtT = sb("qtT", [P, IT, P], bf16)
        qxT = sb("qxT", [P, DC, P], bf16)
        sc = sb("sc", [P, 8])
        flat = ctxt[:, :, :].rearrange("p t d -> p (t d)")
        t_g, t_u, t_v, t_m = (flat[:, i * I:(i + 1) * I] for i in range(4))
        t_q = flat[:, 4 * I:4 * I + I // 2].bitcast(bf16)
        wring = [flat[:, i * D:(i + 1) * D] for i in range(2)]
        wdt = t_u[:, 0:I]
        diag = flat[:, 4 * I + I // 2:4 * I + I // 2 + P]

        ps = ctx.enter_context(nc.psum_tensor("ps", [P, 8, 512], f32))

        def bank16(n, dt):
            return ps[:, n, :].bitcast(dt)

        consts, gin, idx_in = sem("consts"), sem("gin"), sem("idx_in")
        gate_mm, gate_th = sem("gate_mm"), sem("gate_th")
        wrow_in = [sem("wrow_in0"), sem("wrow_in1")]
        wdn_in, wq_ready, wT_mm, wT_sb, wrow_used = (sem(n) for n in ("wdn_in", "wq_ready", "wT_mm", "wT_sb", "wrow_used"))
        dve_s = sem("dve_s")
        x_in, ctx_in = sem("x_in"), sem("ctx_in")
        var_ready, rstd_ready = sem("var_ready"), sem("rstd_ready")
        xl_ready, tp_mm, hi_done, lo_done = sem("xl_ready"), sem("tp_mm"), sem("hi_done"), sem("lo_done")
        vst_done, suf_mm, suf_done = sem("vst_done"), sem("suf_mm"), sem("suf_done")
        stk = [sem("stk0"), sem("stk1")]
        mx_mm, mx_red, m_ready, mT_mm, mrow_ready = (sem(n) for n in ("mx_mm", "mx_red", "m_ready", "mT_mm", "mrow_ready"))
        mrow_in = [sem("mrow_in0"), sem("mrow_in1")]
        w_done, qk_mm, ex_done, pv_done = sem("w_done"), sem("qk_mm"), sem("ex_done"), sem("pv_done")
        o_ev, o_tr, o_done = sem("o_ev"), sem("o_tr"), sem("o_done")
        qx_ready, qxT_mm, qxT_sb = sem("qx_ready"), sem("qxT_mm"), sem("qxT_sb")
        gu_mm, g_sc, th_done, gu_used = sem("gu_mm"), sem("g_sc"), sem("th_done"), sem("gu_used")
        qt_ready, qtT_mm, qtT_sb, dn_mm = sem("qt_ready"), sem("qtT_mm"), sem("qtT_sb"), sem("dn_mm")
        y_done, out_st = sem("y_done"), sem("out_st")

        NTP = QT + NT
        STK = 6 * GH * 16
        XT = QT * 16
        NJ = 2 * IT + DC
        block = ctx.enter_context(nc.Block())

        def put_shift(sp, b, g):
            sp.wait_ge(mrow_ready, b * NG + g + 1)
            for hh in range(GH):
                sp.dma_start(qst[g % 2][ST - 1:ST, hh, :], mrow[hh:hh + 1, g % 2, :]).then_inc(mrow_in[g % 2], 16)

        @block.sync
        def _(sp):
            sp.dma_start(idx[:, :], didx_d.rearrange("(p t) -> p t", t=IT)).then_inc(idx_in, 16)
            sp.dma_start(gates[0:1, 0:1], gx_d.rearrange("(a n) -> a n", a=1)).then_inc(gin, 16)
            sp.dma_start(gates[0:1, 1:2], gf_d.rearrange("(a n) -> a n", a=1)).then_inc(gin, 16)
            for o in range(DC):
                sp.wait_ge(wrow_used, 2 * IT + o)
                sp.dma_start(wdt, wd_d[o * P:(o + 1) * P, :]).then_inc(wdn_in, 16)
            sp.wait_ge(wT_sb, NJ)
            with sp.Fori(0, B) as b:
                sp.dma_start(xs[:, :, :], x_d[b].rearrange("(t p) d -> p t d", p=P)).then_inc(x_in, 16)
                sp.dma_start(ctxt[0:FL, 0:NF, :], ctx_d[b, 0:NEAR, :].rearrange("(t p) d -> p t d", p=FL)).then_inc(ctx_in, 16)
                sp.dma_start(ctxt[:, NF:NT, :], ctx_d[b, NEAR:SK, :].rearrange("(t p) d -> p t d", p=P)).then_inc(ctx_in, 16)
                sp.wait_ge(hi_done, b * NTP + NTP)
                sp.wait_ge(lo_done, b * NTP + NTP)
                for g in range(NG):
                    if g >= 2:
                        sp.wait_ge(pv_done, b * NG * UNITS + (g - 1) * UNITS)
                    for r in range(GH):
                        rows = slice(HD * r, HD * r + HD)
                        for part, (kp, qp) in enumerate(((kTh, qTh), (kTl, qTh), (kTh, qTl))):
                            to = slice(HD * part, HD * part + HD)
                            sp.dma_start(kst[g % 2][to, r, :], kp[rows, g, :]).then_inc(stk[g % 2], 16)
                            sp.dma_start(qst[g % 2][to, r, :], qp[rows, g, :]).then_inc(stk[g % 2], 16)
                    if g >= 1:
                        put_shift(sp, b, g - 1)
                put_shift(sp, b, NG - 1)
                for qt in range(QT):
                    sp.wait_ge(y_done, b * QT + qt + 1)
                    sp.dma_start(out_d[b, qt * P:(qt + 1) * P, :], xs[:, qt, :]).then_inc(out_st, 16)
                sp.wait_ge(out_st, b * XT + XT)
                sp.nop(nofuse=True)

        @block.gpsimd
        def _(pool):
            nc.gpsimd.memset(idf[:, :], 0.0).then_inc(consts, 1)
            pool.wait_ge(consts, 1)
            nc.gpsimd.memset(onesf[:, :], 1.0).then_inc(consts, 1)
            pool.wait_ge(consts, 2)
            nc.gpsimd.memset(maskT[:, :], 0.0).then_inc(consts, 1)
            pool.wait_ge(consts, 3)
            nc.gpsimd.memset(floor[:, :, :], MASKED / SCALE).then_inc(consts, 1)
            pool.wait_ge(consts, 4)
            nc.gpsimd.memset(cneg[:, :], MASKED).then_inc(consts, 1)
            pool.wait_ge(consts, 5)
            nc.gpsimd.memset(half[:, :], -0.5).then_inc(consts, 1)
            pool.wait_ge(consts, 6)
            nc.gpsimd.memset(vst[:, :, :, HD:HD + 1], 1.0).then_inc(consts, 1)
            pool.wait_ge(consts, 7)
            nc.gpsimd.memset(kst[0][ST - 1:ST, :, :], 1.0).then_inc(consts, 1)
            pool.wait_ge(consts, 8)
            nc.gpsimd.memset(kst[1][ST - 1:ST, :, :], 1.0).then_inc(consts, 1)
            pool.wait_ge(consts, 9)
            nc.gpsimd.memset(mch[:, :, :, :], -3.0e38).then_inc(consts, 1)
            pool.wait_ge(consts, 10)
            nc.gpsimd.iota(count[:, :], [[-P, QT]], base=S - 1, channel_multiplier=-1,
                           allow_small_or_imprecise_dtypes=True).then_inc(consts, 1)
            pool.wait_ge(consts, 11)
            nc.gpsimd.affine_select(out=idf[:, :], in_=idf[:, :], compare_op=ALU.not_equal, fill=1.0, base=0,
                                    pattern=[[-1, P]], channel_multiplier=1).then_inc(consts, 1)
            pool.wait_ge(consts, 12)
            nc.gpsimd.affine_select(out=maskT[:, :], in_=maskT[:, :], compare_op=ALU.is_ge, fill=NEG, base=0,
                                    pattern=[[1, P]], channel_multiplier=-1).then_inc(consts, 1)
            pool.wait_ge(consts, 13)
            nc.gpsimd.affine_select(out=later[:, :], in_=onesf[:, :], compare_op=ALU.is_gt, fill=0.0, base=0,
                                    pattern=[[-1, P]], channel_multiplier=1).then_inc(consts, 1)
            pool.wait_ge(consts, 14)
            nc.gpsimd.affine_select(out=floor[:, :, :], in_=floor[:, :, :], compare_op=ALU.is_gt, fill=-3.0e38,
                                    base=S - 1, pattern=[[0, GH], [-P, QT]], channel_multiplier=-1).then_inc(consts, 1)
            pool.wait_ge(consts, 15)
            nc.gpsimd.tensor_copy(idh[:, :], idf[:, :]).then_inc(consts, 1)
            pool.wait_ge(consts, 16)
            nc.gpsimd.tensor_copy(idb[:, :], idf[:, :]).then_inc(consts, 1)
            pool.wait_ge(consts, 17)
            pool.wait_ge(idx_in, 16)
            for j in range(2 * IT):
                if j >= 2:
                    pool.wait_ge(wrow_used, j - 1)
                nc.gpsimd.indirect_dma_start(
                    out=wring[j % 2], out_offset=None, in_=(wg_d if j % 2 == 0 else wu_d)[:, :],
                    in_offset=bass.IndirectOffsetOnAxis(ap=idx[:, j // 2:j // 2 + 1], axis=0)).then_inc(wrow_in[j % 2], 16)
            with pool.Fori(0, B) as b:
                pool.wait_ge(var_ready, 2 * b + 1)
                nc.gpsimd.tensor_tensor(rstd[:, :], ve[:, :], half[:, :], ALU.pow).then_inc(rstd_ready, 1)
                pool.wait_ge(ctx_in, b * 32 + 32)
                pool.nop(nofuse=True)
                for t, (k0, kn) in enumerate(KT):
                    nc.gpsimd.tensor_copy(vst[0:kn, t, :, 0:HD],
                                          ctxt[0:kn, t, :].rearrange("p (h d) -> p h d", h=H)).then_inc(vst_done, 1)
                pool.wait_ge(var_ready, 2 * b + 2)
                nc.gpsimd.tensor_tensor(rstd[:, :], ve[:, :], half[:, :], ALU.pow).then_inc(rstd_ready, 1)

        def act_shift(act, b, g):
            act.wait_ge(m_ready, b * NG + g + 1)
            nc.scalar.activation(w[:, g % 2, :, :], m16[:, g % 2, :, :], ACT.Exp, bias=cneg[:, 0:1],
                                 scale=SCALE).then_inc(w_done, 1)
            act.wait_ge(mT_mm, b * NG + g + 1)
            if g >= 2:
                act.wait_ge(mrow_in[g % 2], b * 2 * GH * 16 + (g // 2) * GH * 16)
            nc.scalar.copy(mrow[:, g % 2, :], bank16(7, f16)[0:GH, 0:S]).then_inc(mrow_ready, 1)

        def act_out(act, b, h):
            act.wait_ge(pv_done, b * NG * UNITS + (h + 1) * NT)
            if h >= 1:
                act.wait_ge(o_tr, b * H + h)
            nc.scalar.copy(oT[:, :], ps[0:HD + 1, 2 + h % 2, :]).then_inc(o_ev, 1)

        @block.scalar
        def _(act):
            act.wait_ge(consts, 17)
            act.wait_ge(gate_mm, 1)
            nc.scalar.activation(tg[:, :], ps[:, 3, 0:2], ACT.Tanh).then_inc(gate_th, 1)
            for j in range(NJ):
                act.wait_ge(wT_mm, j + 1)
                if j < 2 * IT:
                    t, c0 = j // 2, (j % 2) * I
                    nc.scalar.copy(wgu[:, :, c0 + t * P:c0 + (t + 1) * P],
                                   bank16(6, bf16)[:, 0:D].rearrange("p (c n) -> p c n", c=DC))
                    nc.scalar.copy(wsb[:, c0 + t * P:c0 + (t + 1) * P], ps[:, 4, 0:P]).then_inc(wT_sb, 1)
                else:
                    o = j - 2 * IT
                    nc.scalar.copy(wdn[:, 0:8, o * P:(o + 1) * P],
                                   bank16(6, bf16).rearrange("p (c n) -> p c n", c=8))
                    nc.scalar.copy(wdn[:, 8:IT, o * P:(o + 1) * P],
                                   bank16(7, bf16)[:, 0:(IT - 8) * P].rearrange("p (c n) -> p c n", n=P))
                    nc.scalar.copy(wdb[:, o * P:(o + 1) * P], ps[:, 4, 0:P]).then_inc(wT_sb, 1)
            with act.Fori(0, B) as b:
                for i in range(NTP):
                    act.wait_ge(tp_mm, b * NTP + i + 1)
                    src = ps[:, 6 + i % 2, :].rearrange("p (g n) -> p g n", g=NG)
                    if i < QT:
                        nc.scalar.copy(qTh[:, :, i * P:(i + 1) * P], src).then_inc(hi_done, 1)
                    else:
                        k0, kn = KT[i - QT]
                        nc.scalar.copy(kTh[:, :, k0:k0 + kn], src[:, :, 0:kn]).then_inc(hi_done, 1)
                for qt in range(QT):
                    act.wait_ge(suf_mm, b * QT + qt + 1)
                    nc.scalar.copy(suf[:, qt, :], ps[:, 2 + qt % 2, :]).then_inc(suf_done, 1)
                act_shift(act, b, 0)
                for g in range(NG):
                    for u in range(UNITS):
                        hh, t = divmod(u, NT)
                        q0 = max(0, t - NF) * P
                        kn = KT[t][1]
                        n = g * UNITS + u
                        act.wait_ge(qk_mm, b * NG * UNITS + n + 1)
                        if n >= NP:
                            act.wait_ge(pv_done, b * NG * UNITS + n - NP + 1)
                        nc.scalar.activation(pr[0:kn, n % NP, q0:S], ps[0:kn, n % 2, q0:S], ACT.Exp,
                                             scale=SCALE).then_inc(ex_done, 1)
                        if u == 30 and g + 1 < NG:
                            act_shift(act, b, g + 1)
                        if t == 1 and n >= NT:
                            act_out(act, b, g * GH + hh - 1)
                act_out(act, b, H - 1)
                for qt in range(QT):
                    act.wait_ge(qxT_mm, b * QT + qt + 1)
                    nc.scalar.copy(qxT[:, :, :], bank16(6, bf16)[:, 0:D].rearrange("p (c n) -> p c n", c=DC)).then_inc(qxT_sb, 1)
                    for c in range(GC):
                        n = qt * GC + c
                        act.wait_ge(g_sc, b * QT * GC + n + 1)
                        nc.scalar.activation(t_v[:, c * CW:(c + 1) * CW], t_g[:, c * CW:(c + 1) * CW], ACT.Tanh,
                                             scale=0.5).then_inc(th_done, 1)
                    act.wait_ge(qtT_mm, b * QT + qt + 1)
                    nc.scalar.copy(qtT[:, 0:8, :], bank16(6, bf16).rearrange("p (c n) -> p c n", c=8))
                    nc.scalar.copy(qtT[:, 8:IT, :],
                                   bank16(7, bf16)[:, 0:(IT - 8) * P].rearrange("p (c n) -> p c n", n=P)).then_inc(qtT_sb, 1)

        def max_chunk(pe, b, g, j):
            hh, qt, c, k0, k1 = chunks[j]
            n = g * CH + j
            if j == 0:
                pe.wait_ge(stk[g % 2], b * 2 * STK + (g // 2 + 1) * STK)
            if n >= 2:
                pe.wait_ge(mx_red, b * NG * CH + n - 1)
            bank = 4 + n % 2
            d0 = NEAR + P * qt
            lo, hi = max(k0, d0), min(k1, d0 + P)
            last = nc.tensor.matmul(ps[:, bank, 0:k1 - k0], qst[g % 2][0:ST - 1, hh, qt * P:(qt + 1) * P],
                                    kst[g % 2][0:ST - 1, hh, k0:k1], start=True, stop=(hi <= lo))
            if hi > lo:
                last = nc.tensor.matmul(ps[:, bank, lo - k0:hi - k0], maskT[:, :], idb[:, lo - d0:hi - d0],
                                        start=False, stop=True)
            last.then_inc(mx_mm, 1)

        def shift_rows(pe, b, g):
            pe.wait_ge(m_ready, b * NG + g + 1)
            for qt in range(QT):
                last = nc.tensor.transpose(bank16(7, f16)[0:GH, qt * P:(qt + 1) * P], m16[:, g % 2, :, qt], idh[:, :])
            last.then_inc(mT_mm, 1)

        def score_unit(pe, b, g, u):
            hh, t = divmod(u, NT)
            k0, kn = KT[t]
            n = g * UNITS + u
            q0 = max(0, t - NF) * P
            if n >= 2:
                pe.wait_ge(ex_done, b * NG * UNITS + n - 1)
            last = nc.tensor.matmul(ps[0:kn, n % 2, q0:S], kst[g % 2][:, hh, k0:k0 + kn], qst[g % 2][:, hh, q0:S],
                                    start=True, stop=(t < NF))
            if t >= NF:
                last = nc.tensor.matmul(ps[:, n % 2, q0:q0 + P], idb[:, :], maskT[:, :], start=False, stop=True)
            last.then_inc(qk_mm, 1)

        def value_unit(pe, b, g, u):
            hh, t = divmod(u, NT)
            kn = KT[t][1]
            n = g * UNITS + u
            h = g * GH + hh
            q0 = max(0, t - NF) * P
            if t == 0 and h >= 2:
                pe.wait_ge(o_ev, b * H + h - 1)
            pe.wait_ge(ex_done, b * NG * UNITS + n + 1)
            nc.tensor.matmul(ps[0:HD + 1, 2 + h % 2, q0:S], vst[0:kn, t, h, :], pr[0:kn, n % NP, q0:S],
                             start=(t == 0), stop=(t == NT - 1)).then_inc(pv_done, 1)

        def turn_out(pe, b, h):
            pe.wait_ge(o_ev, b * H + h + 1)
            if h >= 1:
                pe.wait_ge(o_done, b * H + h)
            pe.nop(nofuse=True)
            for qt in range(QT):
                last = nc.tensor.transpose(ps[:, 6, qt * (HD + 1):(qt + 1) * (HD + 1)],
                                           oT[:, qt * P:(qt + 1) * P], idf[0:HD + 1, 0:HD + 1])
            last.then_inc(o_tr, 1)

        def ffn_tile(pe, b, qt):
            pe.wait_ge(qx_ready, b * QT + qt + 1)
            for c in range(DC):
                last = nc.tensor.transpose(bank16(6, bf16)[:, c * P:(c + 1) * P], t_q[:, c * P:(c + 1) * P], idb[:, :])
            last.then_inc(qxT_mm, 1)
            pe.wait_ge(qxT_sb, b * QT + qt + 1)
            for c in range(GC):
                n = qt * GC + c
                if n >= 2:
                    pe.wait_ge(gu_used, b * QT * GC + n - 1)
                for side in range(2):
                    for k in range(DC):
                        last = nc.tensor.matmul(ps[:, 2 * (n % 2) + side, 0:CW], qxT[:, k, :],
                                                wgu[:, k, side * I + c * CW:side * I + (c + 1) * CW],
                                                start=(k == 0), stop=(k == DC - 1))
                last.then_inc(gu_mm, 1)
            pe.wait_ge(qt_ready, b * QT + qt + 1)
            for c in range(IT):
                last = nc.tensor.transpose(bank16(6 + c // 8, bf16)[:, (c % 8) * P:(c % 8 + 1) * P],
                                           t_q[:, c * P:(c + 1) * P], idb[:, :])
            last.then_inc(qtT_mm, 1)
            pe.wait_ge(qtT_sb, b * QT + qt + 1)
            if qt >= 1:
                pe.wait_ge(y_done, b * QT + qt)
            for c in range(IT):
                last = nc.tensor.matmul(ps[:, 4, :], qtT[:, c, :], wdn[:, c, :], start=(c == 0), stop=(c == IT - 1))
            last.then_inc(dn_mm, 1)

        @block.tensor
        def _(pe):
            pe.wait_ge(consts, 17)
            pe.wait_ge(gin, 32)
            nc.tensor.matmul(ps[:, 3, 0:2], onesf[0:1, :], gates[0:1, :], start=True, stop=True).then_inc(gate_mm, 1)
            for j in range(NJ):
                pe.wait_ge(wq_ready, j + 1)
                if j >= 1:
                    pe.wait_ge(wT_sb, j)
                quant = (t_q[:, 0:D].rearrange("p (c n) -> p c n", c=DC) if j < 2 * IT
                         else t_q.rearrange("p (n c) -> p c n", c=IT))
                for c in range(DC if j < 2 * IT else IT):
                    nc.tensor.transpose(bank16(6 + c // 8, bf16)[:, (c % 8) * P:(c % 8 + 1) * P],
                                        quant[:, c, :], idb[:, :])
                nc.tensor.matmul(ps[:, 4, 0:P], onesf[:, :], diag, start=True, stop=True).then_inc(wT_mm, 1)
            with pe.Fori(0, B) as b:
                for i in range(NTP):
                    if i < QT:
                        pe.wait_ge(xl_ready, b * QT + i + 1)
                        src, kn = xl[:, i % 2, :], P
                    else:
                        if i == QT:
                            pe.wait_ge(ctx_in, b * 32 + 32)
                        kn = KT[i - QT][1]
                        src = ctxt[0:kn, i - QT, :]
                    if i >= 2:
                        pe.wait_ge(lo_done, b * NTP + i - 1)
                    for g in range(NG):
                        last = nc.tensor.transpose(ps[:, 6 + i % 2, g * P:g * P + kn], src[:, g * P:(g + 1) * P],
                                                   idf[0:kn, 0:kn])
                    last.then_inc(tp_mm, 1)
                for qt in range(QT):
                    if qt >= 2:
                        pe.wait_ge(suf_done, b * QT + qt - 1)
                    for i in range(qt, QT):
                        last = nc.tensor.matmul(ps[:, 2 + qt % 2, :], (later if i == qt else onesf)[:, :],
                                                ctxt[:, NF + i, :], start=(i == qt), stop=(i == QT - 1))
                    last.then_inc(suf_mm, 1)
                pe.wait_ge(suf_done, b * QT + QT)
                pe.wait_ge(vst_done, b * NT + NT)
                for j in range(CH):
                    max_chunk(pe, b, 0, j)
                shift_rows(pe, b, 0)
                for g in range(NG):
                    pe.wait_ge(mrow_in[g % 2], b * 2 * GH * 16 + (g // 2 + 1) * GH * 16)
                    for u in range(UNITS + 1):
                        if u < UNITS:
                            score_unit(pe, b, g, u)
                            if g + 1 < NG and u < CH // 2:
                                max_chunk(pe, b, g + 1, 2 * u)
                                max_chunk(pe, b, g + 1, 2 * u + 1)
                            if g + 1 < NG and u == 29:
                                shift_rows(pe, b, g + 1)
                        if u >= 1:
                            value_unit(pe, b, g, u - 1)
                        if u < UNITS and u % NT == 3 and g * GH + u // NT >= 1:
                            turn_out(pe, b, g * GH + u // NT - 1)
                turn_out(pe, b, H - 1)
                for qt in range(QT):
                    ffn_tile(pe, b, qt)

        class Steps:
            def __init__(self, dve, base):
                self.dve, self.base, self.n = dve, base, 0

            def step(self, ins):
                ins.then_inc(dve_s, 1)
                self.n += 1
                return ins

            def settle(self):
                self.dve.wait_ge(dve_s, self.base + self.n)

        def round_fp8(s, out, v, m):
            s.settle()
            s.step(nc.vector.tensor_scalar(m.bitcast(i32), v.bitcast(i32), EXP_BITS, None, ALU.bitwise_and))
            s.settle()
            s.step(nc.vector.tensor_scalar(m, m, MIN_EXP, ROUND, ALU.max, ALU.mult))
            s.settle()
            s.step(nc.vector.tensor_tensor(v, v, m, ALU.add))
            s.settle()
            return nc.vector.tensor_tensor(out, v, m, ALU.subtract)

        BATCH_STEPS = 2 * 2 * QT + 2 * NG + 7 * H + 20 * QT

        def norm_stats(dve, s, b, which):
            for qt in range(QT):
                s.step(nc.vector.bn_stats(stat[:, qt, :], xs[:, qt, :]))
            s.settle()
            dve.nop(nofuse=True)
            for qt in range(QT):
                s.step(nc.vector.bn_aggr(mv[:, qt, :], stat[:, qt, :]))
            s.settle()
            nc.vector.tensor_scalar(ve[:, :], mv[:, :, 1], EPS, None, ALU.add).then_inc(var_ready, 1)
            dve.wait_ge(rstd_ready, 2 * b + which + 1)

        def max_reduce(dve, s, b, g, j):
            hh, qt, c, k0, k1 = chunks[j]
            n = g * CH + j
            dve.wait_ge(mx_mm, b * NG * CH + n + 1)
            nc.vector.tensor_reduce(mch[:, hh, qt, c:c + 1], ps[:, 4 + n % 2, 0:k1 - k0], AX.X, ALU.max).then_inc(mx_red, 1)

        def max_finish(dve, s, b, g):
            dve.wait_ge(mx_red, b * NG * CH + (g + 1) * CH)
            if g >= 1:
                dve.wait_ge(m_ready, b * NG + g)
            s.step(nc.vector.tensor_reduce(mg[:, :, :], mch[:, :, :, :], AX.X, ALU.max))
            s.settle()
            s.step(nc.vector.tensor_tensor(mg[:, :, :], mg[:, :, :], floor[:, :, :], ALU.max))
            s.settle()
            nc.vector.tensor_scalar(m16[:, g % 2, :, :], mg[:, :, :], -1.0, None, ALU.mult).then_inc(m_ready, 1)

        def join_out(dve, s, b, h):
            g, hh = divmod(h, GH)
            cols = slice(h * HD, (h + 1) * HD)
            ww = w[:, g % 2, hh, :]
            got = ps[:, 6, 0:QT * (HD + 1)].rearrange("p (t d) -> p t d", t=QT)
            wide = [P, QT, HD]
            dve.wait_ge(w_done, b * NG + g + 1)
            s.settle()
            s.step(nc.vector.tensor_tensor(den[:, 0, :], ww, count[:, :], ALU.mult))
            s.step(nc.vector.tensor_tensor(cmb[:, 0, :, :], suf[:, :, cols], ww.unsqueeze(2).broadcast_to(wide), ALU.mult))
            dve.wait_ge(o_tr, b * H + h + 1)
            s.settle()
            s.step(nc.vector.tensor_tensor(den[:, 1, :], den[:, 0, :], got[:, :, HD], ALU.add))
            nc.vector.tensor_tensor(cmb[:, 1, :, :], cmb[:, 0, :, :], got[:, :, 0:HD], ALU.add).then_inc(o_done, 1)
            s.settle()
            s.step(nc.vector.reciprocal(den[:, 2, :], den[:, 1, :]))
            s.settle()
            s.step(nc.vector.tensor_scalar(den[:, 0, :], den[:, 2, :], tg[:, 0:1], None, ALU.mult))
            s.settle()
            dve.wait_ge(o_done, b * H + h + 1)
            s.step(nc.vector.tensor_tensor(cmb[:, 0, :, :], cmb[:, 1, :, :],
                                           den[:, 0, :].unsqueeze(2).broadcast_to(wide), ALU.mult))
            s.settle()
            s.step(nc.vector.tensor_tensor(xs[:, :, cols], xs[:, :, cols], cmb[:, 0, :, :], ALU.add))

        def ffn_rows(dve, s, b, qt):
            xc, v = xl[:, 0, :], xl[:, 1, :]
            if qt >= 1:
                dve.wait_ge(y_done, b * QT + qt)
            s.step(nc.vector.tensor_scalar(xc, xs[:, qt, :], mv[:, qt, 0:1], rstd[:, qt:qt + 1], ALU.subtract, ALU.mult))
            s.settle()
            s.step(nc.vector.tensor_reduce(sc[:, 0:1], xc, AX.X, ALU.max, apply_absolute_value=True))
            s.settle()
            s.step(nc.vector.tensor_scalar(sc[:, 1:2], sc[:, 0:1], 1.0 / FP8_MAX, None, ALU.mult))
            s.settle()
            s.step(nc.vector.reciprocal(sc[:, 2:3], sc[:, 1:2]))
            s.step(nc.vector.tensor_scalar(sc[:, 3:4], sc[:, 1:2], 0.5, None, ALU.mult))
            s.settle()
            s.step(nc.vector.tensor_scalar(v, xc, sc[:, 2:3], None, ALU.mult))
            round_fp8(s, t_q[:, 0:D], v, t_m[:, 0:D]).then_inc(qx_ready, 1)
            for c in range(GC):
                n = qt * GC + c
                cols = slice(c * CW, (c + 1) * CW)
                dve.wait_ge(gu_mm, b * QT * GC + n + 1)
                nc.vector.scalar_tensor_tensor(t_g[:, cols], ps[:, 2 * (n % 2), 0:CW], sc[:, 1:2], wsb[:, cols],
                                               ALU.mult, ALU.mult).then_inc(g_sc, 1)
                nc.vector.scalar_tensor_tensor(t_u[:, cols], ps[:, 2 * (n % 2) + 1, 0:CW], sc[:, 3:4],
                                               wsb[:, I + c * CW:I + (c + 1) * CW], ALU.mult, ALU.mult).then_inc(gu_used, 1)
            dve.wait_ge(th_done, b * QT * GC + (qt + 1) * GC)
            dve.wait_ge(g_sc, b * QT * GC + (qt + 1) * GC)
            s.step(nc.vector.scalar_tensor_tensor(t_v, t_v, 1.0, t_g, ALU.add, ALU.mult))
            dve.wait_ge(gu_used, b * QT * GC + (qt + 1) * GC)
            s.settle()
            s.step(nc.vector.tensor_tensor(t_v, t_v, t_u, ALU.mult))
            s.settle()
            s.step(nc.vector.tensor_reduce(sc[:, 4:5], t_v, AX.X, ALU.max, apply_absolute_value=True))
            s.settle()
            s.step(nc.vector.tensor_scalar(sc[:, 5:6], sc[:, 4:5], 1.0 / FP8_MAX, None, ALU.mult))
            s.settle()
            s.step(nc.vector.reciprocal(sc[:, 6:7], sc[:, 5:6]))
            s.step(nc.vector.tensor_scalar(sc[:, 7:8], sc[:, 5:6], tg[:, 1:2], None, ALU.mult))
            s.settle()
            s.step(nc.vector.tensor_scalar(t_v, t_v, sc[:, 6:7], None, ALU.mult))
            round_fp8(s, t_q, t_v, t_m).then_inc(qt_ready, 1)
            dve.wait_ge(dn_mm, b * QT + qt + 1)
            s.step(nc.vector.scalar_tensor_tensor(t_m[:, 0:D], ps[:, 4, :], sc[:, 7:8], wdb[:, :], ALU.mult, ALU.mult))
            s.settle()
            nc.vector.tensor_tensor(xs[:, qt, :], xs[:, qt, :], t_m[:, 0:D], ALU.add).then_inc(y_done, 1)

        @block.vector
        def _(dve):
            dve.wait_ge(consts, 17)
            s = Steps(dve, 0)
            for j in range(NJ):
                if j < 2 * IT:
                    dve.wait_ge(wrow_in[j % 2], 16 * (j // 2 + 1))
                    rows, n = wring[j % 2], D
                else:
                    dve.wait_ge(wdn_in, 16 * (j - 2 * IT + 1))
                    rows, n = wdt, I
                if j >= 1:
                    dve.wait_ge(wT_mm, j)
                v, m = t_v[:, 0:n], t_m[:, 0:n]
                s.step(nc.vector.tensor_reduce(sc[:, 0:1], rows, AX.X, ALU.max, apply_absolute_value=True))
                s.settle()
                s.step(nc.vector.tensor_scalar(sc[:, 1:2], sc[:, 0:1], 1.0 / FP8_MAX, None, ALU.mult))
                s.settle()
                s.step(nc.vector.reciprocal(sc[:, 2:3], sc[:, 1:2]))
                s.settle()
                s.step(nc.vector.tensor_scalar(diag, idf[:, :], sc[:, 1:2], None, ALU.mult))
                nc.vector.tensor_scalar(v, rows, sc[:, 2:3], None, ALU.mult).then_inc(wrow_used, 1)
                dve.wait_ge(wrow_used, j + 1)
                round_fp8(s, t_q[:, 0:n], v, m).then_inc(wq_ready, 1)
            setup = s.n
            with dve.Fori(0, B) as b:
                s = Steps(dve, b * BATCH_STEPS + setup)
                dve.wait_ge(x_in, b * 16 + 16)
                norm_stats(dve, s, b, 0)
                for qt in range(QT):
                    if qt >= 2:
                        dve.wait_ge(tp_mm, b * NTP + qt - 1)
                    nc.vector.tensor_scalar(xl[:, qt % 2, :], xs[:, qt, :], mv[:, qt, 0:1], rstd[:, qt:qt + 1],
                                            ALU.subtract, ALU.mult).then_inc(xl_ready, 1)
                for i in range(NTP):
                    dve.wait_ge(hi_done, b * NTP + i + 1)
                    src = ps[:, 6 + i % 2, :].rearrange("p (g n) -> p g n", g=NG)
                    if i < QT:
                        hi, lo, kn = qTh[:, :, i * P:(i + 1) * P], qTl[:, :, i * P:(i + 1) * P], P
                    else:
                        k0, kn = KT[i - QT]
                        hi, lo = kTh[:, :, k0:k0 + kn], kTl[:, :, k0:k0 + kn]
                    nc.vector.tensor_tensor(lo, src[:, :, 0:kn], hi, ALU.subtract).then_inc(lo_done, 1)
                for j in range(CH):
                    max_reduce(dve, s, b, 0, j)
                max_finish(dve, s, b, 0)
                dve.wait_ge(suf_done, b * QT + QT)
                dve.wait_ge(gate_th, 1)
                for g in range(NG):
                    for u in range(UNITS):
                        if g + 1 < NG and u < CH // 2:
                            max_reduce(dve, s, b, g + 1, 2 * u)
                            max_reduce(dve, s, b, g + 1, 2 * u + 1)
                        if g + 1 < NG and u == CH // 2:
                            max_finish(dve, s, b, g + 1)
                        if u % NT == 4 and g * GH + u // NT >= 1:
                            join_out(dve, s, b, g * GH + u // NT - 1)
                join_out(dve, s, b, H - 1)
                s.settle()
                norm_stats(dve, s, b, 1)
                for qt in range(QT):
                    ffn_rows(dve, s, b, qt)
                assert s.n == BATCH_STEPS, s.n


_INS = ['x', 'ctx_2048', 'g_xattn', 'g_ffn', 'L0_ffn_w_gate', 'L0_ffn_w_up', 'L0_ffn_w_down', 'L0_ffn_down_reorder_index']


def kernel(**inputs):
    import numpy as np
    import concourse.bacc as bacc
    from concourse import mybir as mb
    from concourse.bass_utils import run_bass_kernel_spmd as run

    nc = bacc.Bacc("TRN2", target_bir_lowering=False, num_devices=1)
    arrays, args = {}, []
    for name in _INS:
        a = np.ascontiguousarray(inputs[name])
        arrays[f"in_{name}"] = a
        args.append(nc.dram_tensor(f"in_{name}", a.shape, mb.dt.from_np(a.dtype), kind="ExternalInput").ap())
    out = nc.dram_tensor("out_0", inputs['x'].shape, mb.dt.float32, kind="ExternalOutput").ap()
    flamingo_gated_block(nc, *args, out)
    r = run(nc, [arrays], core_ids=[0])
    return r.results[0]["out_0"]
```

```python
import concourse.bass as bass
from concourse import mybir
from contextlib import ExitStack


def flamingo_gated_block(nc, x_d, ctx_d, gx_d, gf_d, wg_d, wu_d, wd_d, didx_d, out_d):
    nc.disable_value_cache = True
    f32, f16, bf16, i32 = mybir.dt.float32, mybir.dt.float16, mybir.dt.bfloat16, mybir.dt.int32
    ALU = mybir.AluOpType
    ACT = mybir.ActivationFunctionType
    AX = mybir.AxisListType

    B, S, D = x_d.shape
    SK = ctx_d.shape[1]
    I = wg_d.shape[0]
    P = 128
    H = 16
    HD = D // H
    SCALE = HD ** -0.5
    MASKED = -10000.0
    QT = S // P
    NG, GH = 4, 4
    NEAR = SK - S
    NF = 9
    FL = NEAR // NF
    NT = NF + QT
    KT = [(FL * t, FL) for t in range(NF)] + [(NEAR + P * i, P) for i in range(QT)]
    ST = 3 * HD + 1
    IT = I // P
    DC = D // P
    GC = 4
    CW = I // GC
    FP8_MAX = 448.0
    EXP_BITS = 0x7F800000
    MIN_EXP, ROUND = 2.0 ** -6, 1.5 * 2.0 ** 20
    NEG = -1.0e30
    EPS = 1e-5
    VW = 2 * HD + 1
    LAG = 3
    MAX_AT = 14
    UNITS = GH * NT
    CH = 52
    on_dve = [n % 2 == 1 and (n // UNITS == NG - 1 or not MAX_AT <= n % UNITS < MAX_AT + CH // 2)
              for n in range(NG * UNITS)]
    low_at = [sum(on_dve[m] == on_dve[n] for m in range(n + 1)) for n in range(NG * UNITS)]
    DVE_LOW = sum(on_dve)
    POOL_LOW = NG * UNITS - DVE_LOW
    assert NF * FL == NEAR and IT * P == I

    chunks = []
    for hh in range(GH):
        for qt in range(QT):
            end = NEAR + P * (qt + 1)
            for c in range((end + 511) // 512):
                chunks.append((hh, qt, c, 512 * c, min(512 * c + 512, end)))
    assert len(chunks) == CH

    with ExitStack() as ctx:
        def sb(name, shape, dt=f32):
            return ctx.enter_context(nc.sbuf_tensor(name, shape, dt))

        def sem(name):
            return ctx.enter_context(nc.semaphore(name))

        idf = sb("idf", [P, P])
        idh = sb("idh", [P, P], f16)
        idb = sb("idb", [P, P], bf16)
        onesf = sb("onesf", [P, P])
        later = sb("later", [P, P])
        maskT = sb("maskT", [P, P], bf16)
        floor = sb("floor", [P, GH, QT])
        count = sb("count", [P, QT])
        cneg = sb("cneg", [P, 1])
        half = sb("half", [P, QT])
        gates = sb("gates", [1, 2])
        tg = sb("tg", [P, 2])
        idx = sb("idx", [P, IT], i32)
        wgu = sb("wgu", [P, DC, 2 * I], bf16)
        wdn = sb("wdn", [P, IT, D], bf16)
        wsb = sb("wsb", [P, 2 * I])
        wdb = sb("wdb", [P, D])
        xs = sb("xs", [P, QT, D])
        ctxt = sb("ctxt", [P, NT, D])
        vst = sb("vst", [P, NT, H, VW], f16)
        kTh = sb("kTh", [P, NG, SK], f16)
        kTl = sb("kTl", [P, NG, SK], f16)
        qTh = sb("qTh", [P, NG, S], f16)
        qTl = sb("qTl", [P, NG, S], f16)
        kst = [sb(f"kst{i}", [ST, GH, SK], f16) for i in range(2)]
        qst = [sb(f"qst{i}", [ST, GH, S], f16) for i in range(2)]
        suf = sb("suf", [P, QT, D])
        NP, NL = 6, 4
        pr = sb("pr", [P, NP, S])
        prh = pr[:, :, :].bitcast(bf16).rearrange("p n (s two) -> p n s two", two=2)[:, :, :, 1]
        prl = sb("prl", [P, NL, S], f16)
        oT = sb("oT", [VW, S])
        stat = sb("stat", [P, QT, 6])
        mv = sb("mv", [P, QT, 2])
        ve = sb("ve", [P, QT])
        rstd = sb("rstd", [P, QT])
        mch = sb("mch", [P, GH, QT, 4])
        mg = sb("mg", [P, GH, QT])
        m16 = sb("m16", [P, 2, GH, QT], f16)
        mrow = sb("mrow", [GH, 2, S], f16)
        w = sb("w", [P, 2, GH, QT])
        cmb = sb("cmb", [P, 2, QT, HD])
        den = sb("den", [P, 3, QT])
        qtT = prl[:, 0:3, :].bitcast(bf16).rearrange("p a b -> p (a b)")[:, 0:IT * P].rearrange("p (c n) -> p c n", c=IT)
        qxT = sb("qxT", [P, DC, P], bf16)
        scs = sb("scs", [P, 2, 8])
        sc = scs[:, 0, :]
        qx = pr[:, 2, :].bitcast(bf16).rearrange("p (n d) -> p n d", n=2)
        flat = ctxt[:, :, :].rearrange("p t d -> p (t d)")
        t_g, t_u, t_v, t_m = (flat[:, i * I:(i + 1) * I] for i in range(4))
        t_q = flat[:, 4 * I:4 * I + I // 2].bitcast(bf16)
        wring = [flat[:, i * D:(i + 1) * D] for i in range(2)]
        wdt = t_u[:, 0:I]
        diag = flat[:, 4 * I + I // 2:4 * I + I // 2 + P]

        ps = ctx.enter_context(nc.psum_tensor("ps", [P, 8, 512], f32))

        def bank16(n, dt):
            return ps[:, n, :].bitcast(dt)

        consts, gin, idx_in = sem("consts"), sem("gin"), sem("idx_in")
        gate_mm, gate_th = sem("gate_mm"), sem("gate_th")
        wrow_in = [sem("wrow_in0"), sem("wrow_in1")]
        wdn_in, wq_ready, wT_mm, wT_sb, wrow_used = (sem(n) for n in ("wdn_in", "wq_ready", "wT_mm", "wT_sb", "wrow_used"))
        dve_s = sem("dve_s")
        x_in, ctx_in = sem("x_in"), sem("ctx_in")
        var_ready, rstd_ready = sem("var_ready"), sem("rstd_ready")
        xl_ready, tp_mm, hi_done, lo_done = sem("xl_ready"), sem("tp_mm"), sem("hi_done"), sem("lo_done")
        vh_done, low_pool, low_dve = sem("vh_done"), sem("low_pool"), sem("low_dve")
        vst_done, suf_mm, suf_done = sem("vst_done"), sem("suf_mm"), sem("suf_done")
        stk = [sem("stk0"), sem("stk1")]
        mx_mm, mx_red, m_ready, mT_mm, mrow_ready = (sem(n) for n in ("mx_mm", "mx_red", "m_ready", "mT_mm", "mrow_ready"))
        mrow_in = [sem("mrow_in0"), sem("mrow_in1")]
        w_done, qk_mm, ex_done, pv_done = sem("w_done"), sem("qk_mm"), sem("ex_done"), sem("pv_done")
        o_ev, o_tr, o_done = sem("o_ev"), sem("o_tr"), sem("o_done")
        qx_ready, qxT_mm, qxT_sb = sem("qx_ready"), sem("qxT_mm"), sem("qxT_sb")
        gu_mm, g_sc, th_done, gu_used = sem("gu_mm"), sem("g_sc"), sem("th_done"), sem("gu_used")
        qt_ready, qtT_mm, qtT_sb, dn_mm = sem("qt_ready"), sem("qtT_mm"), sem("qtT_sb"), sem("dn_mm")
        y_done, out_st = sem("y_done"), sem("out_st")

        NTP = QT + NT
        STK = 6 * GH * 16
        XT = QT * 16
        NJ = 2 * IT + DC
        block = ctx.enter_context(nc.Block())

        def put_shift(sp, b, g):
            sp.wait_ge(mrow_ready, b * NG + g + 1)
            for hh in range(GH):
                sp.dma_start(qst[g % 2][ST - 1:ST, hh, :], mrow[hh:hh + 1, g % 2, :]).then_inc(mrow_in[g % 2], 16)

        def put_stacks(sp, b, g):
            if g >= 2:
                sp.wait_ge(pv_done, b * NG * UNITS + (g - 1) * UNITS)
            for part, (kp, qp) in enumerate(((kTh, qTh), (kTl, qTh), (kTh, qTl))):
                to = slice(HD * part, HD * part + HD)
                for r in range(GH):
                    rows = slice(HD * r, HD * r + HD)
                    sp.dma_start(kst[g % 2][to, r, :], kp[rows, g, :]).then_inc(stk[g % 2], 16)
                    sp.dma_start(qst[g % 2][to, r, :], qp[rows, g, :]).then_inc(stk[g % 2], 16)

        @block.sync
        def _(sp):
            sp.dma_start(idx[:, :], didx_d.rearrange("(p t) -> p t", t=IT)).then_inc(idx_in, 16)
            sp.dma_start(gates[0:1, 0:1], gx_d.rearrange("(a n) -> a n", a=1)).then_inc(gin, 16)
            sp.dma_start(gates[0:1, 1:2], gf_d.rearrange("(a n) -> a n", a=1)).then_inc(gin, 16)
            for o in range(DC):
                sp.wait_ge(wrow_used, 2 * IT + o)
                sp.dma_start(wdt, wd_d[o * P:(o + 1) * P, :]).then_inc(wdn_in, 16)
            sp.wait_ge(wT_sb, NJ)
            with sp.Fori(0, B) as b:
                sp.dma_start(xs[:, :, :], x_d[b].rearrange("(t p) d -> p t d", p=P)).then_inc(x_in, 16)
                sp.dma_start(ctxt[0:FL, 0:NF, :], ctx_d[b, 0:NEAR, :].rearrange("(t p) d -> p t d", p=FL)).then_inc(ctx_in, 16)
                sp.dma_start(ctxt[:, NF:NT, :], ctx_d[b, NEAR:SK, :].rearrange("(t p) d -> p t d", p=P)).then_inc(ctx_in, 16)
                sp.wait_ge(hi_done, b * NTP + NTP)
                sp.wait_ge(lo_done, b * NTP + NTP)
                put_stacks(sp, b, 0)
                put_stacks(sp, b, 1)
                put_shift(sp, b, 0)
                put_shift(sp, b, 1)
                for g in range(2, NG):
                    put_stacks(sp, b, g)
                    put_shift(sp, b, g)
                for qt in range(QT):
                    sp.wait_ge(y_done, b * QT + qt + 1)
                    sp.dma_start(out_d[b, qt * P:(qt + 1) * P, :], xs[:, qt, :]).then_inc(out_st, 16)
                sp.wait_ge(out_st, b * XT + XT)
                sp.nop(nofuse=True)

        @block.gpsimd
        def _(pool):
            nc.gpsimd.memset(idf[:, :], 0.0).then_inc(consts, 1)
            pool.wait_ge(consts, 1)
            nc.gpsimd.memset(onesf[:, :], 1.0).then_inc(consts, 1)
            pool.wait_ge(consts, 2)
            nc.gpsimd.memset(maskT[:, :], 0.0).then_inc(consts, 1)
            pool.wait_ge(consts, 3)
            nc.gpsimd.memset(floor[:, :, :], MASKED / SCALE).then_inc(consts, 1)
            pool.wait_ge(consts, 4)
            nc.gpsimd.memset(cneg[:, :], MASKED).then_inc(consts, 1)
            pool.wait_ge(consts, 5)
            nc.gpsimd.memset(half[:, :], -0.5).then_inc(consts, 1)
            pool.wait_ge(consts, 6)
            nc.gpsimd.memset(vst[:, :, :, 2 * HD:VW], 1.0).then_inc(consts, 1)
            pool.wait_ge(consts, 7)
            nc.gpsimd.memset(kst[0][ST - 1:ST, :, :], 1.0).then_inc(consts, 1)
            pool.wait_ge(consts, 8)
            nc.gpsimd.memset(kst[1][ST - 1:ST, :, :], 1.0).then_inc(consts, 1)
            pool.wait_ge(consts, 9)
            nc.gpsimd.memset(mch[:, :, :, :], -3.0e38).then_inc(consts, 1)
            pool.wait_ge(consts, 10)
            nc.gpsimd.iota(count[:, :], [[-P, QT]], base=S - 1, channel_multiplier=-1,
                           allow_small_or_imprecise_dtypes=True).then_inc(consts, 1)
            pool.wait_ge(consts, 11)
            nc.gpsimd.affine_select(out=idf[:, :], in_=idf[:, :], compare_op=ALU.not_equal, fill=1.0, base=0,
                                    pattern=[[-1, P]], channel_multiplier=1).then_inc(consts, 1)
            pool.wait_ge(consts, 12)
            nc.gpsimd.affine_select(out=maskT[:, :], in_=maskT[:, :], compare_op=ALU.is_ge, fill=NEG, base=0,
                                    pattern=[[1, P]], channel_multiplier=-1).then_inc(consts, 1)
            pool.wait_ge(consts, 13)
            nc.gpsimd.affine_select(out=later[:, :], in_=onesf[:, :], compare_op=ALU.is_gt, fill=0.0, base=0,
                                    pattern=[[-1, P]], channel_multiplier=1).then_inc(consts, 1)
            pool.wait_ge(consts, 14)
            nc.gpsimd.affine_select(out=floor[:, :, :], in_=floor[:, :, :], compare_op=ALU.is_gt, fill=-3.0e38,
                                    base=S - 1, pattern=[[0, GH], [-P, QT]], channel_multiplier=-1).then_inc(consts, 1)
            pool.wait_ge(consts, 15)
            nc.gpsimd.tensor_copy(idh[:, :], idf[:, :]).then_inc(consts, 1)
            pool.wait_ge(consts, 16)
            nc.gpsimd.tensor_copy(idb[:, :], idf[:, :]).then_inc(consts, 1)
            pool.wait_ge(consts, 17)
            pool.wait_ge(idx_in, 16)
            for j in range(2 * IT):
                if j >= 2:
                    pool.wait_ge(wrow_used, j - 1)
                nc.gpsimd.indirect_dma_start(
                    out=wring[j % 2], out_offset=None, in_=(wg_d if j % 2 == 0 else wu_d)[:, :],
                    in_offset=bass.IndirectOffsetOnAxis(ap=idx[:, j // 2:j // 2 + 1], axis=0)).then_inc(wrow_in[j % 2], 16)
            with pool.Fori(0, B) as b:
                pool.wait_ge(var_ready, 2 * b + 1)
                nc.gpsimd.tensor_tensor(rstd[:, :], ve[:, :], half[:, :], ALU.pow).then_inc(rstd_ready, 1)
                for t, (k0, kn) in enumerate(KT):
                    pool.wait_ge(vh_done, b * NT + t + 1)
                    nc.gpsimd.tensor_tensor(vst[0:kn, t, :, HD:2 * HD],
                                            ctxt[0:kn, t, :].rearrange("p (h d) -> p h d", h=H),
                                            vst[0:kn, t, :, 0:HD], ALU.subtract).then_inc(vst_done, 1)
                for n in range(NG * UNITS):
                    if on_dve[n]:
                        continue
                    t = n % NT
                    q0 = max(0, t - NF) * P
                    kn = KT[t][1]
                    if n >= NL:
                        pool.wait_ge(pv_done, b * NG * UNITS + n - NL + 1)
                    pool.wait_ge(ex_done, b * NG * UNITS + n + 1)
                    nc.gpsimd.tensor_tensor(prl[0:kn, n % NL, q0:S], pr[0:kn, n % NP, q0:S], prh[0:kn, n % NP, q0:S],
                                            ALU.subtract).then_inc(low_pool, 1)
                pool.wait_ge(var_ready, 2 * b + 2)
                nc.gpsimd.tensor_tensor(rstd[:, :], ve[:, :], half[:, :], ALU.pow).then_inc(rstd_ready, 1)

        def act_shift(act, b, g):
            act.wait_ge(m_ready, b * NG + g + 1)
            nc.scalar.activation(w[:, g % 2, :, :], m16[:, g % 2, :, :], ACT.Exp, bias=cneg[:, 0:1],
                                 scale=SCALE).then_inc(w_done, 1)
            act.wait_ge(mT_mm, b * NG + g + 1)
            if g >= 2:
                act.wait_ge(mrow_in[g % 2], b * 2 * GH * 16 + (g // 2) * GH * 16)
            nc.scalar.copy(mrow[:, g % 2, :], bank16(7, f16)[0:GH, 0:S]).then_inc(mrow_ready, 1)

        def act_out(act, b, h):
            act.wait_ge(pv_done, b * NG * UNITS + (h + 1) * NT)
            if h >= 1:
                act.wait_ge(o_tr, b * H + h)
            nc.scalar.copy(oT[:, :], ps[0:VW, 2 + h % 2, :]).then_inc(o_ev, 1)

        def turn_rows(act, b, qt):
            act.wait_ge(qxT_mm, b * QT + qt + 1)
            if qt >= 1:
                act.wait_ge(gu_mm, b * QT * GC + qt * GC)
            nc.scalar.copy(qxT[:, :, :], bank16(5, bf16)[:, 0:D].rearrange("p (c n) -> p c n", c=DC)).then_inc(qxT_sb, 1)

        def turn_hidden(act, b, qt):
            act.wait_ge(qtT_mm, b * QT + qt + 1)
            if qt >= 1:
                act.wait_ge(dn_mm, b * QT + qt)
            nc.scalar.copy(qtT[:, 0:8, :], bank16(6, bf16).rearrange("p (c n) -> p c n", c=8))
            nc.scalar.copy(qtT[:, 8:IT, :],
                           bank16(7, bf16)[:, 0:(IT - 8) * P].rearrange("p (c n) -> p c n", n=P)).then_inc(qtT_sb, 1)

        @block.scalar
        def _(act):
            act.wait_ge(consts, 17)
            act.wait_ge(gate_mm, 1)
            nc.scalar.activation(tg[:, :], ps[:, 3, 0:2], ACT.Tanh).then_inc(gate_th, 1)
            for j in range(NJ):
                act.wait_ge(wT_mm, j + 1)
                if j < 2 * IT:
                    t, c0 = j // 2, (j % 2) * I
                    nc.scalar.copy(wgu[:, :, c0 + t * P:c0 + (t + 1) * P],
                                   bank16(6, bf16)[:, 0:D].rearrange("p (c n) -> p c n", c=DC))
                    nc.scalar.copy(wsb[:, c0 + t * P:c0 + (t + 1) * P], ps[:, 4, 0:P]).then_inc(wT_sb, 1)
                else:
                    o = j - 2 * IT
                    nc.scalar.copy(wdn[:, 0:8, o * P:(o + 1) * P],
                                   bank16(6, bf16).rearrange("p (c n) -> p c n", c=8))
                    nc.scalar.copy(wdn[:, 8:IT, o * P:(o + 1) * P],
                                   bank16(7, bf16)[:, 0:(IT - 8) * P].rearrange("p (c n) -> p c n", n=P))
                    nc.scalar.copy(wdb[:, o * P:(o + 1) * P], ps[:, 4, 0:P]).then_inc(wT_sb, 1)
            with act.Fori(0, B) as b:
                for i in range(NTP):
                    act.wait_ge(tp_mm, b * NTP + i + 1)
                    src = ps[:, 6 + i % 2, :].rearrange("p (g n) -> p g n", g=NG)
                    if i < QT:
                        nc.scalar.copy(qTh[:, :, i * P:(i + 1) * P], src).then_inc(hi_done, 1)
                    else:
                        k0, kn = KT[i - QT]
                        nc.scalar.copy(kTh[:, :, k0:k0 + kn], src[:, :, 0:kn]).then_inc(hi_done, 1)
                for t, (k0, kn) in enumerate(KT):
                    nc.scalar.copy(vst[0:kn, t, :, 0:HD],
                                   ctxt[0:kn, t, :].rearrange("p (h d) -> p h d", h=H)).then_inc(vh_done, 1)
                for qt in range(QT):
                    act.wait_ge(suf_mm, b * QT + qt + 1)
                    nc.scalar.copy(suf[:, qt, :], ps[:, 2 + qt % 2, :]).then_inc(suf_done, 1)
                act_shift(act, b, 0)
                for g in range(NG):
                    for u in range(UNITS):
                        hh, t = divmod(u, NT)
                        q0 = max(0, t - NF) * P
                        kn = KT[t][1]
                        n = g * UNITS + u
                        act.wait_ge(qk_mm, b * NG * UNITS + n + 1)
                        if n >= NP:
                            act.wait_ge(pv_done, b * NG * UNITS + n - NP + 1)
                        nc.scalar.activation(pr[0:kn, n % NP, q0:S], ps[0:kn, n % 2, q0:S], ACT.Exp,
                                             scale=SCALE).then_inc(ex_done, 1)
                        if u == MAX_AT + CH // 2 + 2 and g + 1 < NG:
                            act_shift(act, b, g + 1)
                        if t == LAG and n >= NT:
                            act_out(act, b, g * GH + hh - 1)
                act_out(act, b, H - 1)
                turn_rows(act, b, 0)
                for qt in range(QT):
                    for c in range(GC):
                        n = qt * GC + c
                        act.wait_ge(g_sc, b * QT * GC + n + 1)
                        if qt >= 1 and c == 0:
                            act.wait_ge(qt_ready, b * QT + qt)
                        nc.scalar.activation(t_v[:, c * CW:(c + 1) * CW], t_g[:, c * CW:(c + 1) * CW], ACT.Tanh,
                                             scale=0.5).then_inc(th_done, 1)
                    if qt >= 1:
                        turn_hidden(act, b, qt - 1)
                    if qt + 1 < QT:
                        turn_rows(act, b, qt + 1)
                turn_hidden(act, b, QT - 1)

        def max_chunk(pe, b, g, j):
            hh, qt, c, k0, k1 = chunks[j]
            n = g * CH + j
            if j == 0:
                pe.wait_ge(stk[g % 2], b * 2 * STK + (g // 2 + 1) * STK)
            if n >= 2:
                pe.wait_ge(mx_red, b * NG * CH + n - 1)
            bank = 4 + n % 2
            d0 = NEAR + P * qt
            lo, hi = max(k0, d0), min(k1, d0 + P)
            last = nc.tensor.matmul(ps[:, bank, 0:k1 - k0], qst[g % 2][0:ST - 1, hh, qt * P:(qt + 1) * P],
                                    kst[g % 2][0:ST - 1, hh, k0:k1], start=True, stop=(hi <= lo))
            if hi > lo:
                last = nc.tensor.matmul(ps[:, bank, lo - k0:hi - k0], maskT[:, :], idb[:, lo - d0:hi - d0],
                                        start=False, stop=True)
            last.then_inc(mx_mm, 1)

        def shift_rows(pe, b, g):
            pe.wait_ge(m_ready, b * NG + g + 1)
            for qt in range(QT):
                last = nc.tensor.transpose(bank16(7, f16)[0:GH, qt * P:(qt + 1) * P], m16[:, g % 2, :, qt], idh[:, :])
            last.then_inc(mT_mm, 1)

        def score_unit(pe, b, g, u):
            hh, t = divmod(u, NT)
            k0, kn = KT[t]
            n = g * UNITS + u
            q0 = max(0, t - NF) * P
            if n >= 2:
                pe.wait_ge(ex_done, b * NG * UNITS + n - 1)
            last = nc.tensor.matmul(ps[0:kn, n % 2, q0:S], kst[g % 2][:, hh, k0:k0 + kn], qst[g % 2][:, hh, q0:S],
                                    start=True, stop=(t < NF))
            if t >= NF:
                last = nc.tensor.matmul(ps[:, n % 2, q0:q0 + P], idb[:, :], maskT[:, :], start=False, stop=True)
            last.then_inc(qk_mm, 1)

        def value_unit(pe, b, g, u):
            hh, t = divmod(u, NT)
            kn = KT[t][1]
            n = g * UNITS + u
            h = g * GH + hh
            q0 = max(0, t - NF) * P
            if t == 0 and h >= 2:
                pe.wait_ge(o_ev, b * H + h - 1)
            if on_dve[n]:
                pe.wait_ge(low_dve, b * DVE_LOW + low_at[n])
            else:
                pe.wait_ge(low_pool, b * POOL_LOW + low_at[n])
            for part, exps in enumerate((prh[0:kn, n % NP, q0:S], prl[0:kn, n % NL, q0:S])):
                last = nc.tensor.matmul(ps[0:VW, 2 + h % 2, q0:S], vst[0:kn, t, h, :], exps,
                                        start=(t == 0 and part == 0), stop=(t == NT - 1 and part == 1))
            last.then_inc(pv_done, 1)

        def turn_out(pe, b, h):
            pe.wait_ge(o_ev, b * H + h + 1)
            if h >= 1:
                pe.wait_ge(o_done, b * H + h)
            pe.nop(nofuse=True)
            for qt in range(QT):
                last = nc.tensor.transpose(ps[:, 6, qt * VW:(qt + 1) * VW],
                                           oT[:, qt * P:(qt + 1) * P], idf[0:VW, 0:VW])
            last.then_inc(o_tr, 1)

        def ffn_turn(pe, b, qt):
            pe.wait_ge(qx_ready, b * QT + qt + 1)
            if qt >= 1:
                pe.wait_ge(qxT_sb, b * QT + qt)
            for c in range(DC):
                last = nc.tensor.transpose(bank16(5, bf16)[:, c * P:(c + 1) * P], qx[:, qt % 2, c * P:(c + 1) * P],
                                           idb[:, :])
            last.then_inc(qxT_mm, 1)

        def ffn_up(pe, b, qt):
            pe.wait_ge(qxT_sb, b * QT + qt + 1)
            for c in range(GC):
                n = qt * GC + c
                if n >= 2:
                    pe.wait_ge(gu_used, b * QT * GC + n - 1)
                for side in range(2):
                    for k in range(DC):
                        last = nc.tensor.matmul(ps[:, 2 * (n % 2) + side, 0:CW], qxT[:, k, :],
                                                wgu[:, k, side * I + c * CW:side * I + (c + 1) * CW],
                                                start=(k == 0), stop=(k == DC - 1))
                last.then_inc(gu_mm, 1)

        def ffn_down(pe, b, qt):
            pe.wait_ge(qt_ready, b * QT + qt + 1)
            if qt >= 1:
                pe.wait_ge(qtT_sb, b * QT + qt)
            for c in range(IT):
                last = nc.tensor.transpose(bank16(6 + c // 8, bf16)[:, (c % 8) * P:(c % 8 + 1) * P],
                                           t_q[:, c * P:(c + 1) * P], idb[:, :])
            last.then_inc(qtT_mm, 1)
            pe.wait_ge(qtT_sb, b * QT + qt + 1)
            if qt >= 1:
                pe.wait_ge(y_done, b * QT + qt)
            for c in range(IT):
                last = nc.tensor.matmul(ps[:, 4, :], qtT[:, c, :], wdn[:, c, :], start=(c == 0), stop=(c == IT - 1))
            last.then_inc(dn_mm, 1)

        @block.tensor
        def _(pe):
            pe.wait_ge(consts, 17)
            pe.wait_ge(gin, 32)
            nc.tensor.matmul(ps[:, 3, 0:2], onesf[0:1, :], gates[0:1, :], start=True, stop=True).then_inc(gate_mm, 1)
            for j in range(NJ):
                pe.wait_ge(wq_ready, j + 1)
                if j >= 1:
                    pe.wait_ge(wT_sb, j)
                quant = (t_q[:, 0:D].rearrange("p (c n) -> p c n", c=DC) if j < 2 * IT
                         else t_q.rearrange("p (n c) -> p c n", c=IT))
                for c in range(DC if j < 2 * IT else IT):
                    nc.tensor.transpose(bank16(6 + c // 8, bf16)[:, (c % 8) * P:(c % 8 + 1) * P],
                                        quant[:, c, :], idb[:, :])
                nc.tensor.matmul(ps[:, 4, 0:P], onesf[:, :], diag, start=True, stop=True).then_inc(wT_mm, 1)
            with pe.Fori(0, B) as b:
                for i in range(NTP):
                    if i < QT:
                        pe.wait_ge(xl_ready, b * QT + i + 1)
                        src, kn = pr[:, i % 2, :], P
                    else:
                        if i == QT:
                            pe.wait_ge(ctx_in, b * 32 + 32)
                        kn = KT[i - QT][1]
                        src = ctxt[0:kn, i - QT, :]
                    if i >= 2:
                        pe.wait_ge(lo_done, b * NTP + i - 1)
                    for g in range(NG):
                        last = nc.tensor.transpose(ps[:, 6 + i % 2, g * P:g * P + kn], src[:, g * P:(g + 1) * P],
                                                   idf[0:kn, 0:kn])
                    last.then_inc(tp_mm, 1)
                for qt in range(QT):
                    if qt >= 2:
                        pe.wait_ge(suf_done, b * QT + qt - 1)
                    for i in range(qt, QT):
                        last = nc.tensor.matmul(ps[:, 2 + qt % 2, :], (later if i == qt else onesf)[:, :],
                                                ctxt[:, NF + i, :], start=(i == qt), stop=(i == QT - 1))
                    last.then_inc(suf_mm, 1)
                pe.wait_ge(suf_done, b * QT + QT)
                pe.wait_ge(vst_done, b * NT + NT)
                for j in range(CH):
                    max_chunk(pe, b, 0, j)
                shift_rows(pe, b, 0)
                for g in range(NG):
                    pe.wait_ge(mrow_in[g % 2], b * 2 * GH * 16 + (g // 2 + 1) * GH * 16)
                    for u in range(UNITS + LAG):
                        if u < UNITS:
                            score_unit(pe, b, g, u)
                            if g + 1 < NG and 0 <= u - MAX_AT < CH // 2:
                                max_chunk(pe, b, g + 1, 2 * (u - MAX_AT))
                                max_chunk(pe, b, g + 1, 2 * (u - MAX_AT) + 1)
                            if g + 1 < NG and u == MAX_AT + CH // 2 + 2:
                                shift_rows(pe, b, g + 1)
                        if u >= LAG:
                            value_unit(pe, b, g, u - LAG)
                        if u < UNITS and u % NT == LAG + 3 and g * GH + u // NT >= 1:
                            turn_out(pe, b, g * GH + u // NT - 1)
                turn_out(pe, b, H - 1)
                ffn_turn(pe, b, 0)
                for qt in range(QT):
                    ffn_up(pe, b, qt)
                    if qt >= 1:
                        ffn_down(pe, b, qt - 1)
                    if qt + 1 < QT:
                        ffn_turn(pe, b, qt + 1)
                ffn_down(pe, b, QT - 1)

        class Steps:
            def __init__(self, dve, base):
                self.dve, self.base, self.n = dve, base, 0

            def step(self, ins):
                ins.then_inc(dve_s, 1)
                self.n += 1
                return ins

            def settle(self):
                self.dve.wait_ge(dve_s, self.base + self.n)

        def round_fp8(s, out, v, m):
            s.settle()
            s.step(nc.vector.tensor_scalar(m.bitcast(i32), v.bitcast(i32), EXP_BITS, None, ALU.bitwise_and))
            s.settle()
            s.step(nc.vector.tensor_scalar(m, m, MIN_EXP, ROUND, ALU.max, ALU.mult))
            s.settle()
            s.step(nc.vector.tensor_tensor(v, v, m, ALU.add))
            s.settle()
            return nc.vector.tensor_tensor(out, v, m, ALU.subtract)

        BATCH_STEPS = 2 * 2 * QT + 2 * NG + 8 * H + 20 * QT

        def norm_stats(dve, s, b, which):
            for qt in range(QT):
                s.step(nc.vector.bn_stats(stat[:, qt, :], xs[:, qt, :]))
            s.settle()
            dve.nop(nofuse=True)
            for qt in range(QT):
                s.step(nc.vector.bn_aggr(mv[:, qt, :], stat[:, qt, :]))
            s.settle()
            nc.vector.tensor_scalar(ve[:, :], mv[:, :, 1], EPS, None, ALU.add).then_inc(var_ready, 1)
            dve.wait_ge(rstd_ready, 2 * b + which + 1)

        def max_reduce(dve, s, b, g, j):
            hh, qt, c, k0, k1 = chunks[j]
            n = g * CH + j
            dve.wait_ge(mx_mm, b * NG * CH + n + 1)
            nc.vector.tensor_reduce(mch[:, hh, qt, c:c + 1], ps[:, 4 + n % 2, 0:k1 - k0], AX.X, ALU.max).then_inc(mx_red, 1)

        def low_part(dve, b, n):
            t = n % NT
            q0, kn = max(0, t - NF) * P, KT[t][1]
            if n >= NL:
                dve.wait_ge(pv_done, b * NG * UNITS + n - NL + 1)
            dve.wait_ge(ex_done, b * NG * UNITS + n + 1)
            nc.vector.tensor_tensor(prl[0:kn, n % NL, q0:S], pr[0:kn, n % NP, q0:S], prh[0:kn, n % NP, q0:S],
                                    ALU.subtract).then_inc(low_dve, 1)

        def max_finish(dve, s, b, g):
            dve.wait_ge(mx_red, b * NG * CH + (g + 1) * CH)
            if g >= 1:
                dve.wait_ge(m_ready, b * NG + g)
            s.step(nc.vector.tensor_reduce(mg[:, :, :], mch[:, :, :, :], AX.X, ALU.max))
            s.settle()
            s.step(nc.vector.tensor_tensor(mg[:, :, :], mg[:, :, :], floor[:, :, :], ALU.max))
            s.settle()
            nc.vector.tensor_scalar(m16[:, g % 2, :, :], mg[:, :, :], -1.0, None, ALU.mult).then_inc(m_ready, 1)

        def join_out(dve, s, b, h):
            g, hh = divmod(h, GH)
            cols = slice(h * HD, (h + 1) * HD)
            ww = w[:, g % 2, hh, :]
            got = ps[:, 6, 0:QT * VW].rearrange("p (t d) -> p t d", t=QT)
            wide = [P, QT, HD]
            dve.wait_ge(w_done, b * NG + g + 1)
            s.settle()
            s.step(nc.vector.tensor_tensor(den[:, 0, :], ww, count[:, :], ALU.mult))
            s.step(nc.vector.tensor_tensor(cmb[:, 0, :, :], suf[:, :, cols], ww.unsqueeze(2).broadcast_to(wide), ALU.mult))
            dve.wait_ge(o_tr, b * H + h + 1)
            s.settle()
            s.step(nc.vector.tensor_tensor(den[:, 1, :], den[:, 0, :], got[:, :, 2 * HD], ALU.add))
            s.step(nc.vector.tensor_tensor(cmb[:, 1, :, :], cmb[:, 0, :, :], got[:, :, 0:HD], ALU.add))
            s.settle()
            nc.vector.tensor_tensor(cmb[:, 1, :, :], cmb[:, 1, :, :], got[:, :, HD:2 * HD], ALU.add).then_inc(o_done, 1)
            s.settle()
            s.step(nc.vector.reciprocal(den[:, 2, :], den[:, 1, :]))
            s.settle()
            s.step(nc.vector.tensor_scalar(den[:, 0, :], den[:, 2, :], tg[:, 0:1], None, ALU.mult))
            s.settle()
            dve.wait_ge(o_done, b * H + h + 1)
            s.step(nc.vector.tensor_tensor(cmb[:, 0, :, :], cmb[:, 1, :, :],
                                           den[:, 0, :].unsqueeze(2).broadcast_to(wide), ALU.mult))
            s.settle()
            s.step(nc.vector.tensor_tensor(xs[:, :, cols], xs[:, :, cols], cmb[:, 0, :, :], ALU.add))

        def ffn_rows(dve, s, b, qt):
            xc, v, m, sc = pr[:, 0, :], pr[:, 1, :], pr[:, 3, :], scs[:, qt % 2, :]
            if qt >= 1:
                dve.wait_ge(qx_ready, b * QT + qt)
            if qt >= 2:
                dve.wait_ge(qxT_mm, b * QT + qt - 1)
            s.step(nc.vector.tensor_scalar(xc, xs[:, qt, :], mv[:, qt, 0:1], rstd[:, qt:qt + 1], ALU.subtract, ALU.mult))
            s.settle()
            s.step(nc.vector.tensor_reduce(sc[:, 0:1], xc, AX.X, ALU.max, apply_absolute_value=True))
            s.settle()
            s.step(nc.vector.tensor_scalar(sc[:, 1:2], sc[:, 0:1], 1.0 / FP8_MAX, None, ALU.mult))
            s.settle()
            s.step(nc.vector.reciprocal(sc[:, 2:3], sc[:, 1:2]))
            s.step(nc.vector.tensor_scalar(sc[:, 3:4], sc[:, 1:2], 0.5, None, ALU.mult))
            s.settle()
            s.step(nc.vector.tensor_scalar(v, xc, sc[:, 2:3], None, ALU.mult))
            round_fp8(s, qx[:, qt % 2, :], v, m).then_inc(qx_ready, 1)

        def ffn_scaled(dve, b, qt):
            sc = scs[:, qt % 2, :]
            for c in range(GC):
                n = qt * GC + c
                cols = slice(c * CW, (c + 1) * CW)
                dve.wait_ge(gu_mm, b * QT * GC + n + 1)
                nc.vector.scalar_tensor_tensor(t_g[:, cols], ps[:, 2 * (n % 2), 0:CW], sc[:, 1:2], wsb[:, cols],
                                               ALU.mult, ALU.mult).then_inc(g_sc, 1)
                nc.vector.scalar_tensor_tensor(t_u[:, cols], ps[:, 2 * (n % 2) + 1, 0:CW], sc[:, 3:4],
                                               wsb[:, I + c * CW:I + (c + 1) * CW], ALU.mult, ALU.mult).then_inc(gu_used, 1)

        def ffn_hidden(dve, s, b, qt):
            sc = scs[:, qt % 2, :]
            dve.wait_ge(th_done, b * QT * GC + (qt + 1) * GC)
            dve.wait_ge(g_sc, b * QT * GC + (qt + 1) * GC)
            s.step(nc.vector.scalar_tensor_tensor(t_v, t_v, 1.0, t_g, ALU.add, ALU.mult))
            dve.wait_ge(gu_used, b * QT * GC + (qt + 1) * GC)
            s.settle()
            s.step(nc.vector.tensor_tensor(t_v, t_v, t_u, ALU.mult))
            s.settle()
            s.step(nc.vector.tensor_reduce(sc[:, 4:5], t_v, AX.X, ALU.max, apply_absolute_value=True))
            s.settle()
            s.step(nc.vector.tensor_scalar(sc[:, 5:6], sc[:, 4:5], 1.0 / FP8_MAX, None, ALU.mult))
            s.settle()
            s.step(nc.vector.reciprocal(sc[:, 6:7], sc[:, 5:6]))
            s.step(nc.vector.tensor_scalar(sc[:, 7:8], sc[:, 5:6], tg[:, 1:2], None, ALU.mult))
            s.settle()
            if qt >= 1:
                dve.wait_ge(qtT_mm, b * QT + qt)
            s.step(nc.vector.tensor_scalar(t_v, t_v, sc[:, 6:7], None, ALU.mult))
            round_fp8(s, t_q, t_v, t_m).then_inc(qt_ready, 1)

        def ffn_out(dve, s, b, qt):
            sc, y = scs[:, qt % 2, :], pr[:, 4, :]
            if qt >= 1:
                dve.wait_ge(y_done, b * QT + qt)
            dve.wait_ge(dn_mm, b * QT + qt + 1)
            s.step(nc.vector.scalar_tensor_tensor(y, ps[:, 4, :], sc[:, 7:8], wdb[:, :], ALU.mult, ALU.mult))
            s.settle()
            nc.vector.tensor_tensor(xs[:, qt, :], xs[:, qt, :], y, ALU.add).then_inc(y_done, 1)

        @block.vector
        def _(dve):
            dve.wait_ge(consts, 17)
            s = Steps(dve, 0)
            for j in range(NJ):
                if j < 2 * IT:
                    dve.wait_ge(wrow_in[j % 2], 16 * (j // 2 + 1))
                    rows, n = wring[j % 2], D
                else:
                    dve.wait_ge(wdn_in, 16 * (j - 2 * IT + 1))
                    rows, n = wdt, I
                if j >= 1:
                    dve.wait_ge(wT_mm, j)
                v, m = t_v[:, 0:n], t_m[:, 0:n]
                s.step(nc.vector.tensor_reduce(sc[:, 0:1], rows, AX.X, ALU.max, apply_absolute_value=True))
                s.settle()
                s.step(nc.vector.tensor_scalar(sc[:, 1:2], sc[:, 0:1], 1.0 / FP8_MAX, None, ALU.mult))
                s.settle()
                s.step(nc.vector.reciprocal(sc[:, 2:3], sc[:, 1:2]))
                s.settle()
                s.step(nc.vector.tensor_scalar(diag, idf[:, :], sc[:, 1:2], None, ALU.mult))
                nc.vector.tensor_scalar(v, rows, sc[:, 2:3], None, ALU.mult).then_inc(wrow_used, 1)
                dve.wait_ge(wrow_used, j + 1)
                round_fp8(s, t_q[:, 0:n], v, m).then_inc(wq_ready, 1)
            setup = s.n
            with dve.Fori(0, B) as b:
                s = Steps(dve, b * BATCH_STEPS + setup)
                dve.wait_ge(x_in, b * 16 + 16)
                norm_stats(dve, s, b, 0)
                for qt in range(QT):
                    if qt >= 2:
                        dve.wait_ge(tp_mm, b * NTP + qt - 1)
                    nc.vector.tensor_scalar(pr[:, qt % 2, :], xs[:, qt, :], mv[:, qt, 0:1], rstd[:, qt:qt + 1],
                                            ALU.subtract, ALU.mult).then_inc(xl_ready, 1)
                for i in range(NTP):
                    dve.wait_ge(hi_done, b * NTP + i + 1)
                    src = ps[:, 6 + i % 2, :].rearrange("p (g n) -> p g n", g=NG)
                    if i < QT:
                        hi, lo, kn = qTh[:, :, i * P:(i + 1) * P], qTl[:, :, i * P:(i + 1) * P], P
                    else:
                        k0, kn = KT[i - QT]
                        hi, lo = kTh[:, :, k0:k0 + kn], kTl[:, :, k0:k0 + kn]
                    nc.vector.tensor_tensor(lo, src[:, :, 0:kn], hi, ALU.subtract).then_inc(lo_done, 1)
                for j in range(CH):
                    max_reduce(dve, s, b, 0, j)
                max_finish(dve, s, b, 0)
                dve.wait_ge(suf_done, b * QT + QT)
                dve.wait_ge(gate_th, 1)
                for g in range(NG):
                    for u in range(UNITS + 1):
                        if g + 1 < NG and 0 <= u - MAX_AT < CH // 2:
                            max_reduce(dve, s, b, g + 1, 2 * (u - MAX_AT))
                            max_reduce(dve, s, b, g + 1, 2 * (u - MAX_AT) + 1)
                        if g + 1 < NG and u == MAX_AT + CH // 2:
                            max_finish(dve, s, b, g + 1)
                        if u >= 1 and on_dve[g * UNITS + u - 1]:
                            low_part(dve, b, g * UNITS + u - 1)
                        if u < UNITS and u % NT == LAG + 4 and g * GH + u // NT >= 1:
                            join_out(dve, s, b, g * GH + u // NT - 1)
                join_out(dve, s, b, H - 1)
                s.settle()
                norm_stats(dve, s, b, 1)
                ffn_rows(dve, s, b, 0)
                for qt in range(QT):
                    ffn_scaled(dve, b, qt)
                    if qt + 1 < QT:
                        ffn_rows(dve, s, b, qt + 1)
                    ffn_hidden(dve, s, b, qt)
                    if qt >= 1:
                        ffn_out(dve, s, b, qt - 1)
                ffn_out(dve, s, b, QT - 1)
                assert s.n == BATCH_STEPS, s.n


_INS = ['x', 'ctx_2048', 'g_xattn', 'g_ffn', 'L0_ffn_w_gate', 'L0_ffn_w_up', 'L0_ffn_w_down', 'L0_ffn_down_reorder_index']


def kernel(**inputs):
    import numpy as np
    import concourse.bacc as bacc
    from concourse import mybir as mb
    from concourse.bass_utils import run_bass_kernel_spmd as run

    nc = bacc.Bacc("TRN2", target_bir_lowering=False, num_devices=1)
    arrays, args = {}, []
    for name in _INS:
        a = np.ascontiguousarray(inputs[name])
        arrays[f"in_{name}"] = a
        args.append(nc.dram_tensor(f"in_{name}", a.shape, mb.dt.from_np(a.dtype), kind="ExternalInput").ap())
    out = nc.dram_tensor("out_0", inputs['x'].shape, mb.dt.float32, kind="ExternalOutput").ap()
    flamingo_gated_block(nc, *args, out)
    r = run(nc, [arrays], core_ids=[0])
    return r.results[0]["out_0"]
```

```python
import concourse.bass as bass
from concourse import mybir
from contextlib import ExitStack


def flamingo_gated_block(nc, x_d, ctx_d, gx_d, gf_d, wg_d, wu_d, wd_d, didx_d, out_d):
    nc.disable_value_cache = True
    f32, f16, bf16, i32 = mybir.dt.float32, mybir.dt.float16, mybir.dt.bfloat16, mybir.dt.int32
    ALU = mybir.AluOpType
    ACT = mybir.ActivationFunctionType
    AX = mybir.AxisListType

    B, S, D = x_d.shape
    SK = ctx_d.shape[1]
    I = wg_d.shape[0]
    P = 128
    H = 16
    HD = D // H
    SCALE = HD ** -0.5
    MASKED = -10000.0
    QT = S // P
    NG, GH = 4, 4
    NEAR = SK - S
    NF = 9
    FL = NEAR // NF
    NT = NF + QT
    KT = [(FL * t, FL) for t in range(NF)] + [(NEAR + P * i, P) for i in range(QT)]
    ST = 3 * HD + 1
    IT = I // P
    DC = D // P
    GC = 4
    CW = I // GC
    FP8_MAX = 448.0
    EXP_BITS = 0x7F800000
    MIN_EXP, ROUND = 2.0 ** -6, 1.5 * 2.0 ** 20
    NEG = -1.0e30
    EPS = 1e-5
    VW = 2 * HD + 1
    LAG = 4
    MAX_AT = 7
    XL_AT = 8
    UNITS = GH * NT
    CH = 52
    on_dve = [n % 2 == 1 and (n // UNITS == NG - 1 or not MAX_AT <= n % UNITS < MAX_AT + CH // 2)
              for n in range(NG * UNITS)]
    low_at = [sum(on_dve[m] == on_dve[n] for m in range(n + 1)) for n in range(NG * UNITS)]
    DVE_LOW = sum(on_dve)
    POOL_LOW = NG * UNITS - DVE_LOW
    assert NF * FL == NEAR and IT * P == I

    chunks = []
    for hh in range(GH):
        for qt in range(QT):
            end = NEAR + P * (qt + 1)
            for c in range((end + 511) // 512):
                chunks.append((hh, qt, c, 512 * c, min(512 * c + 512, end)))
    assert len(chunks) == CH

    with ExitStack() as ctx:
        def sb(name, shape, dt=f32):
            return ctx.enter_context(nc.sbuf_tensor(name, shape, dt))

        def sem(name):
            return ctx.enter_context(nc.semaphore(name))

        idf = sb("idf", [P, P])
        idh = sb("idh", [P, P], f16)
        idb = sb("idb", [P, P], bf16)
        onesf = sb("onesf", [P, P])
        later = sb("later", [P, P])
        maskT = sb("maskT", [P, P], bf16)
        floor = sb("floor", [P, GH, QT])
        count = sb("count", [P, QT])
        cneg = sb("cneg", [P, 1])
        half = sb("half", [P, QT])
        gates = sb("gates", [1, 2])
        tg = sb("tg", [P, 2])
        idx = sb("idx", [P, IT], i32)
        wgu = sb("wgu", [P, DC, 2 * I], bf16)
        wdn = sb("wdn", [P, IT, D], bf16)
        wsb = sb("wsb", [P, 2 * I])
        wdb = sb("wdb", [P, D])
        xs = sb("xs", [P, QT, D])
        ctxt = sb("ctxt", [P, NT, D])
        vsf = sb("vsf", [P, NT * H * VW // 2])
        vst = vsf[:, :].bitcast(f16).rearrange("p (t h d) -> p t h d", t=NT, h=H)
        kf, lf = sb("kf", [P, NG * SK // 2]), sb("lf", [P, NG * SK // 2])
        kTh, kTl = (t[:, :].bitcast(f16).rearrange("p (g n) -> p g n", g=NG) for t in (kf, lf))
        qTh = sb("qTh", [P, NG, S], f16)
        qTl = sb("qTl", [P, NG, S], f16)
        kst = [sb(f"kst{i}", [ST, GH, SK], f16) for i in range(2)]
        qst = [sb(f"qst{i}", [ST, GH, S], f16) for i in range(2)]
        suf = sb("suf", [P, QT, D])
        NP, NL = 6, 4
        pr = sb("pr", [P, NP, S])
        prh = pr[:, :, :].bitcast(bf16).rearrange("p n (s two) -> p n s two", two=2)[:, :, :, 1]
        prl = sb("prl", [P, NL, S], f16)
        oT = sb("oT", [VW, S])
        stat = sb("stat", [P, QT, 6])
        mv = sb("mv", [P, QT, 2])
        ve = sb("ve", [P, QT])
        rstd = sb("rstd", [P, QT])
        mch = sb("mch", [P, GH, QT, 4])
        mg = sb("mg", [P, GH, QT])
        m16 = sb("m16", [P, 2, GH, QT], f16)
        mrow = sb("mrow", [GH, 2, S], f16)
        w = sb("w", [P, 2, GH, QT])
        cmb = sb("cmb", [P, 2, QT, HD])
        den = sb("den", [P, 3, QT])
        qtT = prl[:, 0:3, :].bitcast(bf16).rearrange("p a b -> p (a b)")[:, 0:IT * P].rearrange("p (c n) -> p c n", c=IT)
        qxT = (sb("qxT", [P, DC, P], bf16), prl[:, 3, :].bitcast(bf16).rearrange("p (c n) -> p c n", c=DC))
        scs = sb("scs", [P, QT, 8])
        qx = pr[:, 2, :].bitcast(bf16).rearrange("p (n d) -> p n d", n=2)
        w_g, w_u, w_t, w_r = (vsf[:, i * I:(i + 1) * I] for i in range(4))
        t_g, t_u = (w_g, kf[:, 0:I]), (w_u, kf[:, I:2 * I])
        t_v, t_m = (w_t, lf[:, 0:I]), (w_r, lf[:, I:2 * I])
        t_q = (vsf[:, 4 * I:4 * I + I // 2].bitcast(bf16),
               qTh[:, :, :].rearrange("p g n -> p (g n)").bitcast(bf16)[:, 0:I])
        NR = 6
        wring = [pr[:, i, :] for i in range(NR)]
        wdt = [t[:, i * I:(i + 1) * I] for t in (kf, lf) for i in range(2)]
        w_v, w_m = (w_t, w_u), (w_r, w_g)
        suff = suf[:, :, :].rearrange("p t d -> p (t d)")
        diag = [suff[:, i * P:(i + 1) * P] for i in range(2)]
        w_q = [suff[:, D + i * (I // 2):D + (i + 1) * (I // 2)].bitcast(bf16) for i in range(2)]
        wsc = sb("wsc", [P, 2, 3])

        def weight_job(j):
            if j < 2 * IT:
                rows, n = wring[j % NR], D
            else:
                rows, n = wdt[j - 2 * IT], I
            return rows, w_v[j % 2][:, 0:n], w_m[j % 2][:, 0:n], w_q[j % 2][:, 0:n]

        ps = ctx.enter_context(nc.psum_tensor("ps", [P, 8, 512], f32))

        def bank16(n, dt):
            return ps[:, n, :].bitcast(dt)

        consts, gin, idx_in = sem("consts"), sem("gin"), sem("idx_in")
        gate_mm, gate_th = sem("gate_mm"), sem("gate_th")
        wrow_in = [sem(f"wrow_in{i}") for i in range(NR)]
        wscale_ready, w_added, wdn_in = sem("wscale_ready"), sem("w_added"), [sem(f"wdn_in{o}") for o in range(DC)]
        wq_ready, wT_mm, wT_sb, wrow_used, diag_ready = (sem(n) for n in ("wq_ready", "wT_mm", "wT_sb", "wrow_used", "diag_ready"))
        dve_s = sem("dve_s")
        x_in, ctx_in, ones_in = [sem(f"x_in{t}") for t in range(QT)], sem("ctx_in"), sem("ones_in")
        var_ready, rstd_ready = sem("var_ready"), sem("rstd_ready")
        xl_ready, tp_mm, hi_done, lo_done = sem("xl_ready"), sem("tp_mm"), sem("hi_done"), sem("lo_done")
        vh_done, low_pool, low_dve = sem("vh_done"), sem("low_pool"), sem("low_dve")
        vst_done, suf_mm, suf_done = sem("vst_done"), sem("suf_mm"), sem("suf_done")
        stk = [[sem(f"stk{i}_{r}") for r in range(GH)] for i in range(2)]
        mx_mm, mx_red, m_ready, mT_mm, mrow_ready = (sem(n) for n in ("mx_mm", "mx_red", "m_ready", "mT_mm", "mrow_ready"))
        mrow_in = [sem("mrow_in0"), sem("mrow_in1")]
        w_done, qk_mm, ex_done, pv_done = sem("w_done"), sem("qk_mm"), sem("ex_done"), sem("pv_done")
        o_ev, o_tr, o_done = sem("o_ev"), sem("o_tr"), sem("o_done")
        qx_ready, qxT_mm, qxT_sb = sem("qx_ready"), sem("qxT_mm"), sem("qxT_sb")
        gu_mm, g_sc, th_done = sem("gu_mm"), sem("g_sc"), sem("th_done")
        u_ev, u_sc, gu_ready = sem("u_ev"), sem("u_sc"), sem("gu_ready")
        qx_added, qt_added = sem("qx_added"), sem("qt_added")
        qt_ready, qtT_mm, qtT_sb, dn_mm = sem("qt_ready"), sem("qtT_mm"), sem("qtT_sb"), sem("dn_mm")
        y_done, out_st = sem("y_done"), [sem(f"out_st{t}") for t in range(QT)]

        def max_bank(g, j):
            return ((4, 5, 0, 1)[j % 4], 4) if g == 0 else (4 + j % 2, 2)

        NTP = QT + NT
        STK = 6 * 16
        TB = (6, 7, 0, 1)
        NJ = 2 * IT + DC
        block = ctx.enter_context(nc.Block())

        def put_shift(sp, b, g):
            sp.wait_ge(mrow_ready, b * NG + g + 1)
            for hh in range(GH):
                sp.dma_start(qst[g % 2][ST - 1:ST, hh, :], mrow[hh:hh + 1, g % 2, :]).then_inc(mrow_in[g % 2], 16)

        def put_head(sp, g, r, to, hi, lo, order):
            for part in range(3):
                sp.dma_start(to[g % 2][HD * part:HD * part + HD, r, :],
                             (hi, lo)[order[part]][HD * r:HD * r + HD, g, :]).then_inc(stk[g % 2][r], 16)

        def put_keys(sp, g, r):
            put_head(sp, g, r, kst, kTh, kTl, (0, 1, 0))

        def put_queries(sp, g, r):
            put_head(sp, g, r, qst, qTh, qTl, (0, 0, 1))

        def load_x(sp, b, qt):
            sp.dma_start(xs[:, qt, :], x_d[b, qt * P:(qt + 1) * P, :]).then_inc(x_in[qt], 16)

        def load_context(sp, b):
            sp.dma_start(ctxt[0:FL, 0:NF, :], ctx_d[b, 0:NEAR, :].rearrange("(t p) d -> p t d", p=FL)).then_inc(ctx_in, 16)
            sp.dma_start(ctxt[:, NF:NT, :], ctx_d[b, NEAR:SK, :].rearrange("(t p) d -> p t d", p=P)).then_inc(ctx_in, 16)

        def moves(sp, b, more):
            sp.wait_ge(hi_done, b * NTP + NT)
            sp.wait_ge(lo_done, b * NTP + NT)
            for r in range(GH):
                put_keys(sp, 0, r)
            sp.wait_ge(hi_done, b * NTP + NTP)
            sp.wait_ge(lo_done, b * NTP + NTP)
            for r in range(GH):
                put_queries(sp, 0, r)
            for r in range(GH):
                put_keys(sp, 1, r)
                put_queries(sp, 1, r)
            put_shift(sp, b, 0)
            if more:
                sp.wait_ge(vst_done, b * NT + NT)
                sp.wait_ge(suf_done, b * QT + QT)
                load_context(sp, b + 1)
            put_shift(sp, b, 1)
            for g in range(2, NG):
                for r in range(GH):
                    sp.wait_ge(pv_done, b * NG * UNITS + (g - 2) * UNITS + (r + 1) * NT)
                    put_keys(sp, g, r)
                    put_queries(sp, g, r)
                put_shift(sp, b, g)
            for qt in range(QT + 1):
                if qt < QT:
                    sp.wait_ge(y_done, b * QT + qt + 1)
                    sp.dma_start(out_d[b, qt * P:(qt + 1) * P, :], xs[:, qt, :]).then_inc(out_st[qt], 16)
                if qt >= 1 and more:
                    sp.wait_ge(out_st[qt - 1], b * 16 + 16)
                    load_x(sp, b + 1, qt - 1)

        @block.sync
        def _(sp):
            sp.dma_start(idx[:, :], didx_d.rearrange("(p t) -> p t", t=IT)).then_inc(idx_in, 16)
            sp.dma_start(gates[0:1, 0:1], gx_d.rearrange("(a n) -> a n", a=1)).then_inc(gin, 16)
            sp.dma_start(gates[0:1, 1:2], gf_d.rearrange("(a n) -> a n", a=1)).then_inc(gin, 16)
            sp.wait_ge(wrow_used, 4)
            for o in range(DC):
                sp.dma_start(wdt[o], wd_d[o * P:(o + 1) * P, :]).then_inc(wdn_in[o], 16)
            sp.wait_ge(wrow_used, IT)
            load_context(sp, 0)
            for qt in range(QT):
                load_x(sp, 0, qt)
            with sp.Fori(0, B - 1) as b:
                moves(sp, b, True)
            moves(sp, B - 1, False)
            for qt in range(QT):
                sp.wait_ge(out_st[qt], 16 * B)

        def gather_rows(j):
            nc.gpsimd.indirect_dma_start(
                out=wring[j % NR], out_offset=None, in_=(wg_d if j % 2 == 0 else wu_d)[:, :],
                in_offset=bass.IndirectOffsetOnAxis(ap=idx[:, j // 2:j // 2 + 1], axis=0)).then_inc(wrow_in[j % NR], 16)

        def round_rows(pool, b, qt):
            pool.wait_ge(qx_added, b * QT + qt + 1)
            if qt >= 2:
                pool.wait_ge(qxT_mm, b * QT + qt - 1)
            nc.gpsimd.tensor_tensor(qx[:, qt % 2, :], pr[:, 1, :], pr[:, 3, :], ALU.subtract).then_inc(qx_ready, 1)

        def round_hidden(pool, b, qt):
            pool.wait_ge(qt_added, b * QT + qt + 1)
            if qt >= 2:
                pool.wait_ge(qtT_mm, b * QT + qt - 1)
            nc.gpsimd.tensor_tensor(t_q[qt % 2], t_v[qt % 2], t_m[qt % 2], ALU.subtract).then_inc(qt_ready, 1)

        def gate_up(pool, b, n):
            qt, c = divmod(n, GC)
            cols, u = slice(c * CW, (c + 1) * CW), t_u[qt % 2]
            pool.wait_ge(u_ev, b * QT * GC + n + 1)
            nc.gpsimd.tensor_tensor(u[:, cols], u[:, cols], wsb[:, I + c * CW:I + (c + 1) * CW],
                                    ALU.mult).then_inc(u_sc, 1)
            pool.wait_ge(u_sc, b * QT * GC + n + 1)
            pool.wait_ge(g_sc, b * QT * GC + n + 1)
            nc.gpsimd.tensor_tensor(u[:, cols], u[:, cols], t_g[qt % 2][:, cols], ALU.mult).then_inc(gu_ready, 1)

        @block.gpsimd
        def _(pool):
            nc.gpsimd.memset(idf[:, :], 0.0).then_inc(consts, 1)
            pool.wait_ge(consts, 1)
            nc.gpsimd.memset(onesf[:, :], 1.0).then_inc(consts, 1)
            pool.wait_ge(consts, 2)
            nc.gpsimd.memset(maskT[:, :], 0.0).then_inc(consts, 1)
            pool.wait_ge(consts, 3)
            nc.gpsimd.memset(floor[:, :, :], MASKED / SCALE).then_inc(consts, 1)
            pool.wait_ge(consts, 4)
            nc.gpsimd.memset(cneg[:, :], MASKED).then_inc(consts, 1)
            pool.wait_ge(consts, 5)
            nc.gpsimd.memset(half[:, :], -0.5).then_inc(consts, 1)
            pool.wait_ge(consts, 6)
            nc.gpsimd.memset(kst[0][ST - 1:ST, :, :], 1.0).then_inc(consts, 1)
            pool.wait_ge(consts, 7)
            nc.gpsimd.memset(kst[1][ST - 1:ST, :, :], 1.0).then_inc(consts, 1)
            pool.wait_ge(consts, 8)
            nc.gpsimd.memset(mch[:, :, :, :], -3.0e38).then_inc(consts, 1)
            pool.wait_ge(consts, 9)
            nc.gpsimd.iota(count[:, :], [[-P, QT]], base=S - 1, channel_multiplier=-1,
                           allow_small_or_imprecise_dtypes=True).then_inc(consts, 1)
            pool.wait_ge(consts, 10)
            nc.gpsimd.affine_select(out=idf[:, :], in_=idf[:, :], compare_op=ALU.not_equal, fill=1.0, base=0,
                                    pattern=[[-1, P]], channel_multiplier=1).then_inc(consts, 1)
            pool.wait_ge(consts, 11)
            nc.gpsimd.affine_select(out=maskT[:, :], in_=maskT[:, :], compare_op=ALU.is_ge, fill=NEG, base=0,
                                    pattern=[[1, P]], channel_multiplier=-1).then_inc(consts, 1)
            pool.wait_ge(consts, 12)
            nc.gpsimd.affine_select(out=later[:, :], in_=onesf[:, :], compare_op=ALU.is_gt, fill=0.0, base=0,
                                    pattern=[[-1, P]], channel_multiplier=1).then_inc(consts, 1)
            pool.wait_ge(consts, 13)
            nc.gpsimd.affine_select(out=floor[:, :, :], in_=floor[:, :, :], compare_op=ALU.is_gt, fill=-3.0e38,
                                    base=S - 1, pattern=[[0, GH], [-P, QT]], channel_multiplier=-1).then_inc(consts, 1)
            pool.wait_ge(consts, 14)
            nc.gpsimd.tensor_copy(idh[:, :], idf[:, :]).then_inc(consts, 1)
            pool.wait_ge(consts, 15)
            nc.gpsimd.tensor_copy(idb[:, :], idf[:, :]).then_inc(consts, 1)
            pool.wait_ge(consts, 16)
            pool.wait_ge(idx_in, 16)
            for j in range(NR):
                gather_rows(j)
            for j in range(NJ):
                _, v, m, q = weight_job(j)
                pool.wait_ge(w_added, j + 1)
                if j >= 2:
                    pool.wait_ge(wT_mm, j - 1)
                nc.gpsimd.tensor_tensor(q, v, m, ALU.subtract).then_inc(wq_ready, 1)
                if j + NR < 2 * IT:
                    pool.wait_ge(wrow_used, j + 1)
                    gather_rows(j + NR)
            with pool.Fori(0, B) as b:
                pool.wait_ge(var_ready, 2 * b + 1)
                nc.gpsimd.tensor_tensor(rstd[:, :], ve[:, :], half[:, :], ALU.pow).then_inc(rstd_ready, 1)
                for t, (k0, kn) in enumerate(KT):
                    pool.wait_ge(vh_done, b * NT + t + 1)
                    nc.gpsimd.tensor_tensor(vst[0:kn, t, :, HD:2 * HD],
                                            ctxt[0:kn, t, :].rearrange("p (h d) -> p h d", h=H),
                                            vst[0:kn, t, :, 0:HD], ALU.subtract).then_inc(vst_done, 1)
                nc.gpsimd.memset(vst[:, :, :, 2 * HD:VW], 1.0).then_inc(ones_in, 1)
                for n in range(NG * UNITS):
                    if on_dve[n]:
                        continue
                    t = n % NT
                    q0 = max(0, t - NF) * P
                    kn = KT[t][1]
                    if n >= NL:
                        pool.wait_ge(pv_done, b * NG * UNITS + n - NL + 1)
                    pool.wait_ge(ex_done, b * NG * UNITS + n + 1)
                    nc.gpsimd.tensor_tensor(prl[0:kn, n % NL, q0:S], pr[0:kn, n % NP, q0:S], prh[0:kn, n % NP, q0:S],
                                            ALU.subtract).then_inc(low_pool, 1)
                pool.wait_ge(var_ready, 2 * b + 2)
                nc.gpsimd.tensor_tensor(rstd[:, :], ve[:, :], half[:, :], ALU.pow).then_inc(rstd_ready, 1)
                round_rows(pool, b, 0)
                round_rows(pool, b, 1)
                for qt in range(QT):
                    for c in range(GC):
                        gate_up(pool, b, qt * GC + c)
                    if qt >= 1:
                        round_hidden(pool, b, qt - 1)
                    if qt + 2 < QT:
                        round_rows(pool, b, qt + 2)
                round_hidden(pool, b, QT - 1)

        def weight_scale(act, j):
            rows, v, m, q = weight_job(j)
            act.wait_ge(wscale_ready, j + 1)
            if j >= 2:
                act.wait_ge(wq_ready, j - 1)
            nc.scalar.activation(v, rows, ACT.Copy, scale=wsc[:, j % 2, 2:3]).then_inc(wrow_used, 1)
            if j >= 2:
                act.wait_ge(wT_mm, j - 1)
            nc.scalar.activation(diag[j % 2], idf[:, :], ACT.Copy, scale=wsc[:, j % 2, 1:2]).then_inc(diag_ready, 1)

        def weight_keep(act, j):
            act.wait_ge(wT_mm, j + 1)
            if j < 2 * IT:
                t, c0 = j // 2, (j % 2) * I
                nc.scalar.copy(wgu[:, :, c0 + t * P:c0 + (t + 1) * P],
                               bank16(6 - 2 * (j % 2), bf16)[:, 0:D].rearrange("p (c n) -> p c n", c=DC))
                nc.scalar.copy(wsb[:, c0 + t * P:c0 + (t + 1) * P], ps[:, j % 2, 0:P]).then_inc(wT_sb, 1)
            else:
                o = j - 2 * IT
                nc.scalar.copy(wdn[:, 0:8, o * P:(o + 1) * P],
                               bank16(6 - 2 * (j % 2), bf16).rearrange("p (c n) -> p c n", c=8))
                nc.scalar.copy(wdn[:, 8:IT, o * P:(o + 1) * P],
                               bank16(7 - 2 * (j % 2), bf16)[:, 0:(IT - 8) * P].rearrange("p (c n) -> p c n", n=P))
                nc.scalar.copy(wdb[:, o * P:(o + 1) * P], ps[:, j % 2, 0:P]).then_inc(wT_sb, 1)

        def act_shift(act, b, g):
            act.wait_ge(m_ready, b * NG + g + 1)
            nc.scalar.activation(w[:, g % 2, :, :], m16[:, g % 2, :, :], ACT.Exp, bias=cneg[:, 0:1],
                                 scale=SCALE).then_inc(w_done, 1)
            act.wait_ge(mT_mm, b * NG + g + 1)
            if g >= 2:
                act.wait_ge(mrow_in[g % 2], b * 2 * GH * 16 + (g // 2) * GH * 16)
            nc.scalar.copy(mrow[:, g % 2, :], bank16(7, f16)[0:GH, 0:S]).then_inc(mrow_ready, 1)

        def act_out(act, b, h):
            act.wait_ge(pv_done, b * NG * UNITS + (h + 1) * NT)
            if h >= 1:
                act.wait_ge(o_tr, b * H + h)
            nc.scalar.copy(oT[:, :], ps[0:VW, 2 + h % 2, :]).then_inc(o_ev, 1)

        def turn_rows(act, b, qt):
            act.wait_ge(qxT_mm, b * QT + qt + 1)
            if qt >= 2:
                act.wait_ge(gu_mm, b * QT * GC + (qt - 1) * GC)
            nc.scalar.copy(qxT[qt % 2][:, :, :], bank16(5, bf16)[:, 0:D].rearrange("p (c n) -> p c n", c=DC)).then_inc(qxT_sb, 1)

        def turn_hidden(act, b, qt):
            act.wait_ge(qtT_mm, b * QT + qt + 1)
            if qt >= 1:
                act.wait_ge(dn_mm, b * QT + qt)
            nc.scalar.copy(qtT[:, 0:8, :], bank16(6, bf16).rearrange("p (c n) -> p c n", c=8))
            nc.scalar.copy(qtT[:, 8:IT, :],
                           bank16(7, bf16)[:, 0:(IT - 8) * P].rearrange("p (c n) -> p c n", n=P)).then_inc(qtT_sb, 1)

        @block.scalar
        def _(act):
            act.wait_ge(consts, 16)
            act.wait_ge(gate_mm, 1)
            nc.scalar.activation(tg[:, :], ps[:, 3, 0:2], ACT.Tanh).then_inc(gate_th, 1)
            for j in range(NJ + 1):
                if j < NJ:
                    weight_scale(act, j)
                if j >= 1:
                    weight_keep(act, j - 1)
            with act.Fori(0, B) as b:
                for i in range(NTP):
                    act.wait_ge(tp_mm, b * NTP + i + 1)
                    src = ps[:, TB[i % 4], :].rearrange("p (g n) -> p g n", g=NG)
                    if i >= NT:
                        nc.scalar.copy(qTh[:, :, (i - NT) * P:(i - NT + 1) * P], src).then_inc(hi_done, 1)
                    else:
                        k0, kn = KT[i]
                        nc.scalar.copy(kTh[:, :, k0:k0 + kn], src[:, :, 0:kn]).then_inc(hi_done, 1)
                for t, (k0, kn) in enumerate(KT):
                    nc.scalar.copy(vst[0:kn, t, :, 0:HD],
                                   ctxt[0:kn, t, :].rearrange("p (h d) -> p h d", h=H)).then_inc(vh_done, 1)
                for qt in range(QT):
                    act.wait_ge(suf_mm, b * QT + qt + 1)
                    nc.scalar.copy(suf[:, qt, :], ps[:, 2 + qt % 2, :]).then_inc(suf_done, 1)
                act_shift(act, b, 0)
                for g in range(NG):
                    for u in range(UNITS):
                        hh, t = divmod(u, NT)
                        q0 = max(0, t - NF) * P
                        kn = KT[t][1]
                        n = g * UNITS + u
                        act.wait_ge(qk_mm, b * NG * UNITS + n + 1)
                        if n >= NP:
                            act.wait_ge(pv_done, b * NG * UNITS + n - NP + 1)
                        nc.scalar.activation(pr[0:kn, n % NP, q0:S], ps[0:kn, n % 2, q0:S], ACT.Exp,
                                             scale=SCALE).then_inc(ex_done, 1)
                        if u == MAX_AT + CH // 2 + 2 and g + 1 < NG:
                            act_shift(act, b, g + 1)
                        if t == LAG and n >= NT:
                            act_out(act, b, g * GH + hh - 1)
                act_out(act, b, H - 1)
                turn_rows(act, b, 0)
                turn_rows(act, b, 1)
                for qt in range(QT):
                    for c in range(GC):
                        n = qt * GC + c
                        cols = slice(c * CW, (c + 1) * CW)
                        act.wait_ge(gu_mm, b * QT * GC + n + 1)
                        nc.scalar.activation(t_u[qt % 2][:, cols], ps[:, 2 * (n % 2) + 1, 0:CW], ACT.Copy,
                                             scale=scs[:, qt, 3:4]).then_inc(u_ev, 1)
                        act.wait_ge(g_sc, b * QT * GC + n + 1)
                        if qt >= 2 and c == 0:
                            act.wait_ge(qt_ready, b * QT + qt - 1)
                        nc.scalar.activation(t_v[qt % 2][:, cols], t_g[qt % 2][:, cols], ACT.Tanh,
                                             scale=0.5).then_inc(th_done, 1)
                    if qt >= 1:
                        turn_hidden(act, b, qt - 1)
                    if qt + 2 < QT:
                        turn_rows(act, b, qt + 2)
                turn_hidden(act, b, QT - 1)

        def max_chunk(pe, b, g, j):
            hh, qt, c, k0, k1 = chunks[j]
            n = g * CH + j
            if j % (CH // GH) == 0:
                pe.wait_ge(stk[g % 2][hh], b * 2 * STK + (g // 2 + 1) * STK)
            bank, ring = max_bank(g, j)
            if n >= ring:
                pe.wait_ge(mx_red, b * NG * CH + n - ring + 1)
            d0 = NEAR + P * qt
            lo, hi = max(k0, d0), min(k1, d0 + P)
            last = nc.tensor.matmul(ps[:, bank, 0:k1 - k0], qst[g % 2][0:ST - 1, hh, qt * P:(qt + 1) * P],
                                    kst[g % 2][0:ST - 1, hh, k0:k1], start=True, stop=(hi <= lo))
            if hi > lo:
                last = nc.tensor.matmul(ps[:, bank, lo - k0:hi - k0], maskT[:, :], idb[:, lo - d0:hi - d0],
                                        start=False, stop=True)
            last.then_inc(mx_mm, 1)

        def shift_rows(pe, b, g):
            pe.wait_ge(m_ready, b * NG + g + 1)
            for qt in range(QT):
                last = nc.tensor.transpose(bank16(7, f16)[0:GH, qt * P:(qt + 1) * P], m16[:, g % 2, :, qt], idh[:, :])
            last.then_inc(mT_mm, 1)

        def score_unit(pe, b, g, u):
            hh, t = divmod(u, NT)
            k0, kn = KT[t]
            n = g * UNITS + u
            q0 = max(0, t - NF) * P
            if n >= 2:
                pe.wait_ge(ex_done, b * NG * UNITS + n - 1)
            last = nc.tensor.matmul(ps[0:kn, n % 2, q0:S], kst[g % 2][:, hh, k0:k0 + kn], qst[g % 2][:, hh, q0:S],
                                    start=True, stop=(t < NF))
            if t >= NF:
                last = nc.tensor.matmul(ps[:, n % 2, q0:q0 + P], idb[:, :], maskT[:, :], start=False, stop=True)
            last.then_inc(qk_mm, 1)

        def value_unit(pe, b, g, u):
            hh, t = divmod(u, NT)
            kn = KT[t][1]
            n = g * UNITS + u
            h = g * GH + hh
            q0 = max(0, t - NF) * P
            if t == 0 and h >= 2:
                pe.wait_ge(o_ev, b * H + h - 1)
            if on_dve[n]:
                pe.wait_ge(low_dve, b * DVE_LOW + low_at[n])
            else:
                pe.wait_ge(low_pool, b * POOL_LOW + low_at[n])
            for part, exps in enumerate((prh[0:kn, n % NP, q0:S], prl[0:kn, n % NL, q0:S])):
                last = nc.tensor.matmul(ps[0:VW, 2 + h % 2, q0:S], vst[0:kn, t, h, :], exps,
                                        start=(t == 0 and part == 0), stop=(t == NT - 1 and part == 1))
            last.then_inc(pv_done, 1)

        def turn_out(pe, b, h):
            pe.wait_ge(o_ev, b * H + h + 1)
            if h >= 1:
                pe.wait_ge(o_done, b * H + h)
            pe.nop(nofuse=True)
            for qt in range(QT):
                last = nc.tensor.transpose(ps[:, 6, qt * VW:(qt + 1) * VW],
                                           oT[:, qt * P:(qt + 1) * P], idf[0:VW, 0:VW])
            last.then_inc(o_tr, 1)

        def ffn_turn(pe, b, qt):
            pe.wait_ge(qx_ready, b * QT + qt + 1)
            if qt >= 1:
                pe.wait_ge(qxT_sb, b * QT + qt)
            for c in range(DC):
                last = nc.tensor.transpose(bank16(5, bf16)[:, c * P:(c + 1) * P], qx[:, qt % 2, c * P:(c + 1) * P],
                                           idb[:, :])
            last.then_inc(qxT_mm, 1)

        def ffn_up(pe, b, qt, c0, c1):
            if c0 == 0:
                pe.wait_ge(qxT_sb, b * QT + qt + 1)
            for c in range(c0, c1):
                n = qt * GC + c
                if n >= 2:
                    pe.wait_ge(g_sc, b * QT * GC + n - 1)
                    pe.wait_ge(u_ev, b * QT * GC + n - 1)
                for side in range(2):
                    for k in range(DC):
                        last = nc.tensor.matmul(ps[:, 2 * (n % 2) + side, 0:CW], qxT[qt % 2][:, k, :],
                                                wgu[:, k, side * I + c * CW:side * I + (c + 1) * CW],
                                                start=(k == 0), stop=(k == DC - 1))
                last.then_inc(gu_mm, 1)

        def ffn_hidden_turn(pe, b, qt):
            pe.wait_ge(qt_ready, b * QT + qt + 1)
            if qt >= 1:
                pe.wait_ge(qtT_sb, b * QT + qt)
            for c in range(IT):
                last = nc.tensor.transpose(bank16(6 + c // 8, bf16)[:, (c % 8) * P:(c % 8 + 1) * P],
                                           t_q[qt % 2][:, c * P:(c + 1) * P], idb[:, :])
            last.then_inc(qtT_mm, 1)

        def ffn_down(pe, b, qt):
            pe.wait_ge(qtT_sb, b * QT + qt + 1)
            if qt >= 1:
                pe.wait_ge(y_done, b * QT + qt)
            for c in range(IT):
                last = nc.tensor.matmul(ps[:, 4, :], qtT[:, c, :], wdn[:, c, :], start=(c == 0), stop=(c == IT - 1))
            last.then_inc(dn_mm, 1)

        @block.tensor
        def _(pe):
            pe.wait_ge(consts, 16)
            pe.wait_ge(gin, 32)
            nc.tensor.matmul(ps[:, 3, 0:2], onesf[0:1, :], gates[0:1, :], start=True, stop=True).then_inc(gate_mm, 1)
            for j in range(NJ):
                pe.wait_ge(wq_ready, j + 1)
                if j >= 2:
                    pe.wait_ge(wT_sb, j - 1)
                q = weight_job(j)[3]
                quant = (q.rearrange("p (c n) -> p c n", c=DC) if j < 2 * IT else q.rearrange("p (n c) -> p c n", c=IT))
                for c in range(DC if j < 2 * IT else IT):
                    nc.tensor.transpose(bank16(6 - 2 * (j % 2) + c // 8, bf16)[:, (c % 8) * P:(c % 8 + 1) * P],
                                        quant[:, c, :], idb[:, :])
                pe.wait_ge(diag_ready, j + 1)
                nc.tensor.matmul(ps[:, j % 2, 0:P], onesf[:, :], diag[j % 2], start=True, stop=True).then_inc(wT_mm, 1)
            pe.wait_ge(wT_sb, NJ)
            with pe.Fori(0, B) as b:
                for i in range(NTP):
                    if i < NT:
                        if i == 0:
                            pe.wait_ge(ctx_in, b * 32 + 32)
                        kn = KT[i][1]
                        src = ctxt[0:kn, i, :]
                    else:
                        pe.wait_ge(xl_ready, b * QT + i - NT + 1)
                        src, kn = pr[:, i - NT, :], P
                    if i >= 4:
                        pe.wait_ge(lo_done, b * NTP + i - 3)
                    for g in range(NG):
                        last = nc.tensor.transpose(ps[:, TB[i % 4], g * P:g * P + kn], src[:, g * P:(g + 1) * P],
                                                   idf[0:kn, 0:kn])
                    last.then_inc(tp_mm, 1)
                for qt in range(QT):
                    if qt >= 2:
                        pe.wait_ge(suf_done, b * QT + qt - 1)
                    for i in range(qt, QT):
                        last = nc.tensor.matmul(ps[:, 2 + qt % 2, :], (later if i == qt else onesf)[:, :],
                                                ctxt[:, NF + i, :], start=(i == qt), stop=(i == QT - 1))
                    last.then_inc(suf_mm, 1)
                pe.wait_ge(suf_done, b * QT + QT)
                for j in range(CH):
                    max_chunk(pe, b, 0, j)
                shift_rows(pe, b, 0)
                pe.wait_ge(vst_done, b * NT + NT)
                pe.wait_ge(ones_in, b + 1)
                for g in range(NG):
                    pe.wait_ge(mrow_in[g % 2], b * 2 * GH * 16 + (g // 2 + 1) * GH * 16)
                    for u in range(UNITS + LAG):
                        if u < UNITS:
                            score_unit(pe, b, g, u)
                            if g + 1 < NG and 0 <= u - MAX_AT < CH // 2:
                                max_chunk(pe, b, g + 1, 2 * (u - MAX_AT))
                                max_chunk(pe, b, g + 1, 2 * (u - MAX_AT) + 1)
                            if g + 1 < NG and u == MAX_AT + CH // 2 + 2:
                                shift_rows(pe, b, g + 1)
                        if u >= LAG:
                            value_unit(pe, b, g, u - LAG)
                        if u < UNITS and u % NT == LAG + 3 and g * GH + u // NT >= 1:
                            turn_out(pe, b, g * GH + u // NT - 1)
                turn_out(pe, b, H - 1)
                ffn_turn(pe, b, 0)
                ffn_up(pe, b, 0, 0, 2)
                ffn_turn(pe, b, 1)
                for qt in range(QT):
                    ffn_up(pe, b, qt, 2, GC)
                    if qt >= 2:
                        ffn_down(pe, b, qt - 2)
                    if qt + 1 < QT:
                        ffn_up(pe, b, qt + 1, 0, 2)
                    if qt >= 1:
                        ffn_hidden_turn(pe, b, qt - 1)
                    if qt + 2 < QT:
                        ffn_turn(pe, b, qt + 2)
                ffn_down(pe, b, QT - 2)
                ffn_hidden_turn(pe, b, QT - 1)
                ffn_down(pe, b, QT - 1)

        class Steps:
            def __init__(self, dve, base):
                self.dve, self.base, self.n = dve, base, 0

            def step(self, ins):
                ins.then_inc(dve_s, 1)
                self.n += 1
                return ins

            def settle(self):
                self.dve.wait_ge(dve_s, self.base + self.n)

        def add_round(s, v, m):
            s.step(nc.vector.tensor_scalar(m.bitcast(i32), v.bitcast(i32), EXP_BITS, None, ALU.bitwise_and))
            s.settle()
            s.step(nc.vector.tensor_scalar(m, m, MIN_EXP, ROUND, ALU.max, ALU.mult))
            s.settle()
            return nc.vector.tensor_tensor(v, v, m, ALU.add)

        BATCH_STEPS = 2 * 2 * QT + 2 * NG + 8 * H + 17 * QT

        def weight_stats(dve, s, j):
            rows = weight_job(j)[0]
            if j < 2 * IT:
                dve.wait_ge(wrow_in[j % NR], 16 * (j // NR + 1))
            else:
                dve.wait_ge(wdn_in[j - 2 * IT], 16)
            if j >= 2:
                dve.wait_ge(diag_ready, j - 1)
            s.step(nc.vector.tensor_reduce(wsc[:, j % 2, 0:1], rows, AX.X, ALU.max, apply_absolute_value=True))
            s.settle()
            s.step(nc.vector.tensor_scalar(wsc[:, j % 2, 1:2], wsc[:, j % 2, 0:1], 1.0 / FP8_MAX, None, ALU.mult))
            s.settle()
            nc.vector.reciprocal(wsc[:, j % 2, 2:3], wsc[:, j % 2, 1:2]).then_inc(wscale_ready, 1)

        def weight_round(dve, s, j):
            _, v, m, _ = weight_job(j)
            dve.wait_ge(wrow_used, j + 1)
            if j >= 2:
                dve.wait_ge(wq_ready, j - 1)
            add_round(s, v, m).then_inc(w_added, 1)

        def norm_stats(dve, s, b, which):
            for qt in range(QT):
                if which == 0:
                    dve.wait_ge(x_in[qt], b * 16 + 16)
                s.step(nc.vector.bn_stats(stat[:, qt, :], xs[:, qt, :]))
            s.settle()
            dve.nop(nofuse=True)
            for qt in range(QT):
                s.step(nc.vector.bn_aggr(mv[:, qt, :], stat[:, qt, :]))
            s.settle()
            nc.vector.tensor_scalar(ve[:, :], mv[:, :, 1], EPS, None, ALU.add).then_inc(var_ready, 1)
            dve.wait_ge(rstd_ready, 2 * b + which + 1)

        def max_reduce(dve, s, b, g, j):
            hh, qt, c, k0, k1 = chunks[j]
            n = g * CH + j
            dve.wait_ge(mx_mm, b * NG * CH + n + 1)
            nc.vector.tensor_reduce(mch[:, hh, qt, c:c + 1], ps[:, max_bank(g, j)[0], 0:k1 - k0], AX.X, ALU.max).then_inc(mx_red, 1)

        def low_part(dve, b, n):
            t = n % NT
            q0, kn = max(0, t - NF) * P, KT[t][1]
            if n >= NL:
                dve.wait_ge(pv_done, b * NG * UNITS + n - NL + 1)
            dve.wait_ge(ex_done, b * NG * UNITS + n + 1)
            nc.vector.tensor_tensor(prl[0:kn, n % NL, q0:S], pr[0:kn, n % NP, q0:S], prh[0:kn, n % NP, q0:S],
                                    ALU.subtract).then_inc(low_dve, 1)

        def max_finish(dve, s, b, g):
            dve.wait_ge(mx_red, b * NG * CH + (g + 1) * CH)
            if g >= 1:
                dve.wait_ge(m_ready, b * NG + g)
            s.step(nc.vector.tensor_reduce(mg[:, :, :], mch[:, :, :, :], AX.X, ALU.max))
            s.settle()
            s.step(nc.vector.tensor_tensor(mg[:, :, :], mg[:, :, :], floor[:, :, :], ALU.max))
            s.settle()
            nc.vector.tensor_scalar(m16[:, g % 2, :, :], mg[:, :, :], -1.0, None, ALU.mult).then_inc(m_ready, 1)

        def join_out(dve, s, b, h):
            g, hh = divmod(h, GH)
            cols = slice(h * HD, (h + 1) * HD)
            ww = w[:, g % 2, hh, :]
            got = ps[:, 6, 0:QT * VW].rearrange("p (t d) -> p t d", t=QT)
            wide = [P, QT, HD]
            dve.wait_ge(w_done, b * NG + g + 1)
            s.settle()
            s.step(nc.vector.tensor_tensor(den[:, 0, :], ww, count[:, :], ALU.mult))
            s.step(nc.vector.tensor_tensor(cmb[:, 0, :, :], suf[:, :, cols], ww.unsqueeze(2).broadcast_to(wide), ALU.mult))
            dve.wait_ge(o_tr, b * H + h + 1)
            s.settle()
            s.step(nc.vector.tensor_tensor(den[:, 1, :], den[:, 0, :], got[:, :, 2 * HD], ALU.add))
            s.step(nc.vector.tensor_tensor(cmb[:, 1, :, :], cmb[:, 0, :, :], got[:, :, 0:HD], ALU.add))
            s.settle()
            nc.vector.tensor_tensor(cmb[:, 1, :, :], cmb[:, 1, :, :], got[:, :, HD:2 * HD], ALU.add).then_inc(o_done, 1)
            s.settle()
            s.step(nc.vector.reciprocal(den[:, 2, :], den[:, 1, :]))
            s.settle()
            s.step(nc.vector.tensor_scalar(den[:, 0, :], den[:, 2, :], tg[:, 0:1], None, ALU.mult))
            s.settle()
            dve.wait_ge(o_done, b * H + h + 1)
            s.step(nc.vector.tensor_tensor(cmb[:, 0, :, :], cmb[:, 1, :, :],
                                           den[:, 0, :].unsqueeze(2).broadcast_to(wide), ALU.mult))
            s.settle()
            s.step(nc.vector.tensor_tensor(xs[:, :, cols], xs[:, :, cols], cmb[:, 0, :, :], ALU.add))

        def ffn_rows(dve, s, b, qt):
            xc, v, m, sc = pr[:, 0, :], pr[:, 1, :], pr[:, 3, :], scs[:, qt, :]
            if qt >= 1:
                dve.wait_ge(qx_ready, b * QT + qt)
            s.step(nc.vector.tensor_scalar(xc, xs[:, qt, :], mv[:, qt, 0:1], rstd[:, qt:qt + 1], ALU.subtract, ALU.mult))
            s.settle()
            s.step(nc.vector.tensor_reduce(sc[:, 0:1], xc, AX.X, ALU.max, apply_absolute_value=True))
            s.settle()
            s.step(nc.vector.tensor_scalar(sc[:, 1:2], sc[:, 0:1], 1.0 / FP8_MAX, None, ALU.mult))
            s.settle()
            s.step(nc.vector.reciprocal(sc[:, 2:3], sc[:, 1:2]))
            s.step(nc.vector.tensor_scalar(sc[:, 3:4], sc[:, 1:2], 0.5, None, ALU.mult))
            s.settle()
            s.step(nc.vector.tensor_scalar(v, xc, sc[:, 2:3], None, ALU.mult))
            s.settle()
            add_round(s, v, m).then_inc(qx_added, 1)

        def ffn_scaled(dve, b, qt):
            for c in range(GC):
                n = qt * GC + c
                cols = slice(c * CW, (c + 1) * CW)
                dve.wait_ge(gu_mm, b * QT * GC + n + 1)
                nc.vector.scalar_tensor_tensor(t_g[qt % 2][:, cols], ps[:, 2 * (n % 2), 0:CW], scs[:, qt, 1:2],
                                               wsb[:, cols], ALU.mult, ALU.mult).then_inc(g_sc, 1)

        def ffn_hidden(dve, s, b, qt):
            sc, v = scs[:, qt, :], t_v[qt % 2]
            dve.wait_ge(th_done, b * QT * GC + (qt + 1) * GC)
            dve.wait_ge(gu_ready, b * QT * GC + (qt + 1) * GC)
            s.step(nc.vector.scalar_tensor_tensor(v, v, 1.0, t_u[qt % 2], ALU.add, ALU.mult))
            s.settle()
            s.step(nc.vector.tensor_reduce(sc[:, 4:5], v, AX.X, ALU.max, apply_absolute_value=True))
            s.settle()
            s.step(nc.vector.tensor_scalar(sc[:, 5:6], sc[:, 4:5], 1.0 / FP8_MAX, None, ALU.mult))
            s.settle()
            s.step(nc.vector.reciprocal(sc[:, 6:7], sc[:, 5:6]))
            s.settle()
            s.step(nc.vector.tensor_scalar(sc[:, 7:8], sc[:, 5:6], tg[:, 1:2], None, ALU.mult))

        def ffn_round(dve, s, b, qt):
            v = t_v[qt % 2]
            s.settle()
            s.step(nc.vector.tensor_scalar(v, v, scs[:, qt, 6:7], None, ALU.mult))
            s.settle()
            if qt >= 2:
                dve.wait_ge(qt_ready, b * QT + qt - 1)
            add_round(s, v, t_m[qt % 2]).then_inc(qt_added, 1)

        def ffn_out(dve, s, b, qt):
            sc, y = scs[:, qt, :], pr[:, 4, :]
            if qt >= 1:
                dve.wait_ge(y_done, b * QT + qt)
            dve.wait_ge(dn_mm, b * QT + qt + 1)
            s.step(nc.vector.scalar_tensor_tensor(y, ps[:, 4, :], sc[:, 7:8], wdb[:, :], ALU.mult, ALU.mult))
            s.settle()
            nc.vector.tensor_tensor(xs[:, qt, :], xs[:, qt, :], y, ALU.add).then_inc(y_done, 1)

        @block.vector
        def _(dve):
            dve.wait_ge(consts, 16)
            s = Steps(dve, 0)
            for j in range(NJ + 1):
                if j < NJ:
                    weight_stats(dve, s, j)
                if j >= 1:
                    weight_round(dve, s, j - 1)
            setup = s.n
            with dve.Fori(0, B) as b:
                s = Steps(dve, b * BATCH_STEPS + setup)
                for i in range(NTP):
                    if i == XL_AT:
                        norm_stats(dve, s, b, 0)
                        for qt in range(QT):
                            nc.vector.tensor_scalar(pr[:, qt, :], xs[:, qt, :], mv[:, qt, 0:1], rstd[:, qt:qt + 1],
                                                    ALU.subtract, ALU.mult).then_inc(xl_ready, 1)
                    dve.wait_ge(hi_done, b * NTP + i + 1)
                    src = ps[:, TB[i % 4], :].rearrange("p (g n) -> p g n", g=NG)
                    if i >= NT:
                        cols, kn = slice((i - NT) * P, (i - NT + 1) * P), P
                        hi, lo = qTh[:, :, cols], qTl[:, :, cols]
                    else:
                        k0, kn = KT[i]
                        hi, lo = kTh[:, :, k0:k0 + kn], kTl[:, :, k0:k0 + kn]
                    nc.vector.tensor_tensor(lo, src[:, :, 0:kn], hi, ALU.subtract).then_inc(lo_done, 1)
                for j in range(CH):
                    max_reduce(dve, s, b, 0, j)
                max_finish(dve, s, b, 0)
                dve.wait_ge(suf_done, b * QT + QT)
                dve.wait_ge(gate_th, 1)
                for g in range(NG):
                    for u in range(UNITS + 1):
                        if g + 1 < NG and 0 <= u - MAX_AT < CH // 2:
                            max_reduce(dve, s, b, g + 1, 2 * (u - MAX_AT))
                            max_reduce(dve, s, b, g + 1, 2 * (u - MAX_AT) + 1)
                        if g + 1 < NG and u == MAX_AT + CH // 2:
                            max_finish(dve, s, b, g + 1)
                        if u >= 1 and on_dve[g * UNITS + u - 1]:
                            low_part(dve, b, g * UNITS + u - 1)
                        if u < UNITS and u % NT == LAG + 4 and g * GH + u // NT >= 1:
                            join_out(dve, s, b, g * GH + u // NT - 1)
                join_out(dve, s, b, H - 1)
                s.settle()
                norm_stats(dve, s, b, 1)
                ffn_rows(dve, s, b, 0)
                ffn_rows(dve, s, b, 1)
                for qt in range(QT):
                    ffn_scaled(dve, b, qt)
                    if qt >= 1:
                        ffn_round(dve, s, b, qt - 1)
                    if qt + 2 < QT:
                        ffn_rows(dve, s, b, qt + 2)
                    if qt >= 2:
                        ffn_out(dve, s, b, qt - 2)
                    ffn_hidden(dve, s, b, qt)
                ffn_round(dve, s, b, QT - 1)
                ffn_out(dve, s, b, QT - 2)
                ffn_out(dve, s, b, QT - 1)
                assert s.n == BATCH_STEPS, s.n


_INS = ['x', 'ctx_2048', 'g_xattn', 'g_ffn', 'L0_ffn_w_gate', 'L0_ffn_w_up', 'L0_ffn_w_down', 'L0_ffn_down_reorder_index']


def kernel(**inputs):
    import numpy as np
    import concourse.bacc as bacc
    from concourse import mybir as mb
    from concourse.bass_utils import run_bass_kernel_spmd as run

    nc = bacc.Bacc("TRN2", target_bir_lowering=False, num_devices=1)
    arrays, args = {}, []
    for name in _INS:
        a = np.ascontiguousarray(inputs[name])
        arrays[f"in_{name}"] = a
        args.append(nc.dram_tensor(f"in_{name}", a.shape, mb.dt.from_np(a.dtype), kind="ExternalInput").ap())
    out = nc.dram_tensor("out_0", inputs['x'].shape, mb.dt.float32, kind="ExternalOutput").ap()
    flamingo_gated_block(nc, *args, out)
    r = run(nc, [arrays], core_ids=[0])
    return r.results[0]["out_0"]
```
